# Optimizing a Trainium2 kernel written in Bass

```python
import numpy as np
import jax
import jax.numpy as jnp

def _softmax(x, axis=-1):
    return jax.nn.softmax(x, axis=axis)

def _gelu(x):
    return jax.nn.gelu(x, approximate=True)

def _silu(x):
    return jax.nn.silu(x)

def _sigmoid(x):
    return jax.nn.sigmoid(x)

def _layernorm(x, axis=-1, eps=1e-05):
    m = jnp.mean(x, axis=axis, keepdims=True)
    v = jnp.var(x, axis=axis, keepdims=True)
    return (x - m) / jnp.sqrt(v + eps)

def _scatter_add(tgt, idx, src, axis=0):
    return tgt.at[idx].add(src)

def _segment_sum(src, seg, n):
    return jax.ops.segment_sum(src, seg, n)
kernel_name = 'mk_macaron_d1_jaxref_r8_ab15b7'

def setup_inputs(seed: int=0):
    np.random.seed(seed)
    _w = jnp.asarray

    def _L0_attn_setup():
        import jax, jax.numpy as jnp
        import numpy as np
        B, T, C = (2, 512, 128)
        H, M, CHUNK = (16, 64, 128)
        D = C // H
        DELTA = 1e-06
        key = jax.random.key(seed)
        ks = jax.random.split(key, 4)
        x = jax.random.normal(ks[0], (B, T, C), dtype=jnp.float32)
        Wqkv = jax.random.normal(ks[1], (3 * C, C), dtype=jnp.float32) * 0.02
        bqkv = jnp.zeros((3 * C,), dtype=jnp.float32)
        Wout = jax.random.normal(ks[2], (C, C), dtype=jnp.float32) * 0.02
        bout = jnp.zeros((C,), dtype=jnp.float32)
        proj = jax.random.normal(ks[3], (H, D, M), dtype=jnp.float32) / np.sqrt(D)
        return {'x': x, 'Wqkv': Wqkv, 'bqkv': bqkv, 'Wout': Wout, 'bout': bout, 'proj': proj}
    _L0_attn_in = _L0_attn_setup()

    def _L0_ffn_setup():
        import jax, jax.numpy as jnp
        import numpy as np
        NUM_EXPERTS = 8
        HIDDEN = 128
        D_FF = 512
        SCALE = 0.8
        SPARSITY = 0.1

        def _perturb_attractive(w, scale=SCALE, sparsity=SPARSITY):
            a = jnp.abs(w)
            flat = a.ravel()
            n = flat.shape[0]
            k = max(1, int(n * sparsity / 2))
            s = jnp.sort(flat)
            thr_bot = s[k - 1]
            thr_top = s[n - k]
            tier = jnp.where(a >= thr_top, -1.0, jnp.where(a <= thr_bot, 1.0, 0.0))
            return w + scale * w * tier

        def _stack_expert_params(w):
            pw = _perturb_attractive(w)
            return jnp.concatenate([w[None], jnp.broadcast_to(pw, (NUM_EXPERTS - 1,) + w.shape)], axis=0)
        key = jax.random.key(seed)
        ks = jax.random.split(key, 6)
        B, S, H, F, E = (2, 256, HIDDEN, D_FF, NUM_EXPERTS)
        return {'x': jax.random.normal(ks[0], (B, S, H), dtype=jnp.float32), 'W1': jax.random.normal(ks[1], (H, F), dtype=jnp.float32) * (1.0 / np.sqrt(H)), 'b1': jax.random.normal(ks[2], (F,), dtype=jnp.float32) * 0.02, 'W2': jax.random.normal(ks[3], (F, H), dtype=jnp.float32) * (1.0 / np.sqrt(F)), 'b2': jax.random.normal(ks[4], (H,), dtype=jnp.float32) * 0.02, 'ln_gamma': jnp.ones((H,), dtype=jnp.float32), 'ln_beta': jnp.zeros((H,), dtype=jnp.float32), 'Wr': jax.random.normal(ks[5], (H, E), dtype=jnp.float32) * (1.0 / np.sqrt(H)), 'br': jnp.zeros((E,), dtype=jnp.float32)}
    _L0_ffn_in = _L0_ffn_setup()
    _d = {'L0_attn_x': _L0_attn_in['x'], 'L0_attn_Wqkv': _L0_attn_in['Wqkv'], 'L0_attn_bqkv': _L0_attn_in['bqkv'], 'L0_attn_Wout': _L0_attn_in['Wout'], 'L0_attn_bout': _L0_attn_in['bout'], 'L0_attn_proj': _L0_attn_in['proj'], 'L0_ffn_W1': _L0_ffn_in['W1'], 'L0_ffn_b1': _L0_ffn_in['b1'], 'L0_ffn_W2': _L0_ffn_in['W2'], 'L0_ffn_b2': _L0_ffn_in['b2'], 'L0_ffn_ln_gamma': _L0_ffn_in['ln_gamma'], 'L0_ffn_ln_beta': _L0_ffn_in['ln_beta'], 'L0_ffn_Wr': _L0_ffn_in['Wr'], 'L0_ffn_br': _L0_ffn_in['br']}
    _x0 = _d['L0_attn_x']
    _d['L0_attn_x'] = jax.random.normal(jax.random.fold_in(jax.random.key(seed), 1), (32, 256, 128), dtype=_x0.dtype)
    del _x0
    return _d

def reference(L0_attn_x, L0_attn_Wqkv, L0_attn_bqkv, L0_attn_Wout, L0_attn_bout, L0_attn_proj, L0_ffn_W1, L0_ffn_b1, L0_ffn_W2, L0_ffn_b2, L0_ffn_ln_gamma, L0_ffn_ln_beta, L0_ffn_Wr, L0_ffn_br):

    def _L0_attn_ref(x, Wqkv, bqkv, Wout, bout, proj):
        import jax, jax.numpy as jnp
        import numpy as np
        B, T, C = (2, 512, 128)
        H, M, CHUNK = (16, 64, 128)
        D = C // H
        DELTA = 1e-06
        b, t, c = x.shape
        qkv = x @ Wqkv.T + bqkv
        q, k, v = jnp.split(qkv, 3, axis=-1)

        def to_heads(z):
            return z.reshape(b, t, H, D).transpose(0, 2, 1, 3).astype(jnp.float32)
        q, k, v = (to_heads(q), to_heads(k), to_heads(v))
        nch = t // CHUNK

        def to_chunks(z):
            return z.reshape(b, H, nch, CHUNK, D).transpose(2, 0, 1, 3, 4)
        qc, kc, vc = (to_chunks(q), to_chunks(k), to_chunks(v))
        mask = jnp.tril(jnp.ones((CHUNK, CHUNK), dtype=jnp.float32))

        def step(carry, inp):
            kv_state, k_state = carry
            q_ch, k_ch, v_ch = inp
            qp = jax.nn.relu(jnp.einsum('bhtd,hdm->bhtm', q_ch, proj))
            kp = jax.nn.relu(jnp.einsum('bhtd,hdm->bhtm', k_ch, proj))
            ctx_hist = jnp.einsum('bhtm,bhmd->bhtd', qp, kv_state)
            norm_hist = jnp.einsum('bhtm,bhm->bht', qp, k_state)
            aw = jnp.einsum('bhtm,bhsm->bhts', qp, kp) * mask
            ctx_intra = jnp.einsum('bhts,bhsd->bhtd', aw, v_ch)
            norm_intra = aw.sum(-1)
            out = (ctx_hist + ctx_intra) / (norm_hist + norm_intra + DELTA)[..., None]
            new_kv = kv_state + jnp.einsum('bhtm,bhtd->bhmd', kp, v_ch)
            new_k = k_state + kp.sum(2)
            return ((new_kv, new_k), out)
        carry0 = (jnp.zeros((b, H, M, D), jnp.float32), jnp.zeros((b, H, M), jnp.float32))
        _, outs = jax.lax.scan(step, carry0, (qc, kc, vc))
        out = outs.transpose(1, 2, 0, 3, 4).reshape(b, H, t, D)
        out = out.transpose(0, 2, 1, 3).reshape(b, t, c)
        return out @ Wout.T + bout

    def _L0_ffn_ref(x, W1, b1, W2, b2, ln_gamma, ln_beta, Wr, br):
        import jax, jax.numpy as jnp
        import numpy as np
        NUM_EXPERTS = 8
        HIDDEN = 128
        D_FF = 512
        SCALE = 0.8
        SPARSITY = 0.1

        def _perturb_attractive(w, scale=SCALE, sparsity=SPARSITY):
            a = jnp.abs(w)
            flat = a.ravel()
            n = flat.shape[0]
            k = max(1, int(n * sparsity / 2))
            s = jnp.sort(flat)
            thr_bot = s[k - 1]
            thr_top = s[n - k]
            tier = jnp.where(a >= thr_top, -1.0, jnp.where(a <= thr_bot, 1.0, 0.0))
            return w + scale * w * tier

        def _stack_expert_params(w):
            pw = _perturb_attractive(w)
            return jnp.concatenate([w[None], jnp.broadcast_to(pw, (NUM_EXPERTS - 1,) + w.shape)], axis=0)
        mu = jnp.mean(x, axis=-1, keepdims=True)
        var = jnp.mean(jnp.square(x - mu), axis=-1, keepdims=True)
        h = (x - mu) * jax.lax.rsqrt(var + 1e-05) * ln_gamma + ln_beta
        logits = jnp.einsum('bsh,he->bse', h, Wr) + br
        probs = jax.nn.softmax(logits, axis=-1)
        W1s = _stack_expert_params(W1)
        b1s = _stack_expert_params(b1)
        W2s = _stack_expert_params(W2)
        b2s = _stack_expert_params(b2)
        pre = jnp.einsum('bsh,ehf->besf', x, W1s) + b1s[None, :, None, :]
        act = jax.nn.gelu(pre)
        y = jnp.einsum('besf,efh->besh', act, W2s) + b2s[None, :, None, :]
        out = jnp.einsum('bse,besh->bsh', probs, y)
        return out
    x = L0_attn_x
    x = x + 0.5 * _L0_ffn_ref(_layernorm(x, axis=-1), L0_ffn_W1, L0_ffn_b1, L0_ffn_W2, L0_ffn_b2, L0_ffn_ln_gamma, L0_ffn_ln_beta, L0_ffn_Wr, L0_ffn_br)
    x = x + _L0_attn_ref(_layernorm(x, axis=-1), L0_attn_Wqkv, L0_attn_bqkv, L0_attn_Wout, L0_attn_bout, L0_attn_proj)
    x = x + 0.5 * _L0_ffn_ref(_layernorm(x, axis=-1), L0_ffn_W1, L0_ffn_b1, L0_ffn_W2, L0_ffn_b2, L0_ffn_ln_gamma, L0_ffn_ln_beta, L0_ffn_Wr, L0_ffn_br)
    return x

_drawn_inputs = setup_inputs


def setup_inputs(seed=0):
    import zlib

    import numpy as np

    out = dict(_drawn_inputs(seed))
    spreads = {'L0_attn_bqkv': (0.0, 0.32),
     'L0_attn_bout': (0.0, 0.1),
     'L0_ffn_ln_gamma': (1.0, 0.6),
     'L0_ffn_ln_beta': (0.0, 2.0),
     'L0_ffn_br': (0.0, 2.0)}
    factors = {'L0_attn_Wqkv': 6.019, 'L0_attn_proj': 35.3, 'L0_ffn_b1': 6.437, 'L0_ffn_b2': 3.625}
    for name, (base, spread) in spreads.items():
        noise = np.random.default_rng([zlib.crc32(name.encode()), seed]).standard_normal(out[name].shape)
        drawn = base * np.exp(spread * noise) if base else spread * noise
        out[name] = jnp.asarray(drawn.astype(out[name].dtype))
    for name, factor in factors.items():
        out[name] = (out[name] * factor).astype(out[name].dtype)
    return out
```

```python
import math
from contextlib import ExitStack

import concourse.bass as bass
from concourse import mybir

F32 = mybir.dt.float32
F16 = mybir.dt.float16
I32 = mybir.dt.int32
ALU = mybir.AluOpType
ACT = mybir.ActivationFunctionType
AX_X = mybir.AxisListType.X

P = 128
EPS = 1e-5
DELTA = 1e-6
LOG2E = math.log2(math.e)
SCALE, SPARSITY = 0.8, 0.1


class Steps:

    def __init__(self, eng, sem, before):
        self.eng, self.sem, self.before, self.n = eng, sem, before, 0

    def __call__(self, ins):
        self.n += 1
        ins.then_inc(self.sem, 1)
        self.eng.wait_ge(self.sem, self.before + self.n)


def macaron_kernel(nc, x_in, Wqkv, bqkv, Wout, bout, proj, W1, b1, W2, b2, gamma, beta, Wr, br, out):
    B, S, C = x_in.shape
    H, D, M = proj.shape
    FF = W1.shape[1]
    E = Wr.shape[1]
    G = B * S // P
    SUB = 4
    T = SUB * P
    NT = G // SUB
    NSEQ = T // S
    FC = FF // P
    K2 = 2 * FC
    PAIRS = H // 2
    COMBOS = NSEQ * H
    HG = 4
    GROUPS = H // HG
    VW = 32
    AW = S + P
    assert C == P and H * D == P and S == 2 * P and 2 * M == P and NSEQ == 2 and FC == 4

    x_dram = x_in.rearrange("b (g p) c -> p (b g) c", p=P)
    out_dram = out.rearrange("b (g p) c -> p (b g) c", p=P)

    with ExitStack() as ctx:
        def sb(name, shape, dt=F32):
            return ctx.enter_context(nc.sbuf_tensor(name, shape, dt))

        def bank(name):
            return ctx.enter_context(nc.psum_tensor(name, [P, 512], F32))

        def sem(name):
            return ctx.enter_context(nc.semaphore(name))

        x = sb("x_all", [P, G, C])
        ident = sb("ident", [P, P])
        causal = sb("causal", [P, AW])
        w1 = [sb("w1_clean", [P, FC, P]), sb("w1_perturbed", [P, FC, P])]
        w2 = [sb("w2_clean", [P, FC, P]), sb("w2_perturbed", [P, FC, P])]
        b1c = [sb("b1_clean", [P, FC]), sb("b1_perturbed", [P, FC])]
        b2c = [sb("b2_clean", [P, 1]), sb("b2_perturbed", [P, 1])]
        wqkv_sb = sb("wqkv_sb", [P, 3, C])
        wout_sb = sb("wout_sb", [P, C])
        bqk_sb = sb("bqk_sb", [P, 2])
        proj_bd = sb("proj_blockdiag", [P, H * M])
        wr_sb = sb("wr_sb", [P, E])
        gamma_sb = sb("gamma_sb", [P, 1])
        beta_sb = sb("beta_sb", [P, 1])
        bv_rows = sb("bv_rows", [P, C])
        bout_rows = sb("bout_rows", [P, C])
        br_rows = sb("br_rows", [P, E])
        wv_t = sb("wv_t", [P, C])
        wout_t = sb("wout_t", [P, C])
        feat_w = sb("feat_w", [P, 2, H * M])
        feat_b = sb("feat_b", [P, PAIRS, 2])
        wr_g = sb("wr_g", [P, VW])
        beta_wide = sb("beta_wide", [P, P])
        wr_l = sb("wr_l", [P, E])
        logit_b = sb("logit_b", [P, E])
        a1 = sb("abs_w1", [P, FF])
        a2 = sb("abs_w2", [P, FF])
        ab1 = sb("abs_b1", [P, FC])
        ab2 = sb("abs_b2", [P, 1])
        below = sb("below", [P, 8, FF], F16)
        mask_top = sb("mask_top", [P, FF])
        mask_bot = sb("mask_bot", [P, FF])
        ones16 = sb("ones16", [P, P], F16)
        found = sb("found", [P, 8], I32)
        trial = sb("trial", [P, 8], I32)
        bit = sb("bit", [P, 8], I32)
        keep = sb("keep", [P, 8], I32)
        rank = sb("rank", [P, 8])
        cnt = sb("cnt", [P, 8], F16)
        bn6 = sb("bn6", [P, SUB, 6])
        mv = sb("mean_var", [P, SUB, 2])
        minus_half = sb("minus_half", [P, SUB])
        var_eps = sb("var_eps", [P, SUB])
        eps_tile = sb("eps_tile", [P, SUB])
        spare = sb("spare", [P, 1])
        rstd = sb("rstd", [P, SUB])
        ratio = sb("ratio", [P, SUB])
        rstd2 = sb("rstd2", [P, SUB])
        xn = sb("xn", [P, SUB, C])
        xnT = sb("xnT", [P, T])
        two = sb("two", [P, SUB, E])
        logT = sb("logT", [P, P])
        z = sb("z", [P, SUB, E])
        zmax = sb("zmax", [P, SUB])
        ez = sb("ez", [P, SUB, E])
        esum = sb("esum", [P, SUB])
        etot = sb("etot", [P, SUB])
        erec = sb("erec", [P, SUB])
        prob = sb("prob", [P, 2, SUB])
        hid = [sb(f"hid{i}", [P, T]) for i in range(4)]
        yT = [sb(f"yT{i}", [P, T]) for i in range(2)]
        qf = [sb(f"qf{i}", [P, T]) for i in range(2)]
        kf = [sb(f"kf{i}", [P, T]) for i in range(2)]
        v_aug = sb("v_aug", [P, SUB, H, VW])
        aw = [sb(f"aw{i}", [P, AW]) for i in range(4)]
        ctxT = [sb(f"ctxT{i}", [P, T]) for i in range(2)]
        den = sb("den", [P, SUB, HG])
        rden = sb("rden", [P, SUB, HG])
        ctxn = sb("ctxn", [P, SUB, C])
        ctxnT = sb("ctxnT", [P, T])

        bk = [bank(f"bank{i}") for i in range(8)]
        X_BANK = bk[7]
        H_BANK = [bk[0], bk[1], bk[2]]
        Y_BANK = [bk[3], bk[4]]
        YTOK_BANK = bk[5]
        L_BANK = bk[6]
        Q_BANK, KEY_BANK = bk[0], bk[1]
        S_BANK = [bk[2], bk[3], bk[4]]
        C_BANK = bk[5]
        T_BANK = bk[6]

        w_loaded = sem("w_loaded")
        cols_loaded = sem("cols_loaded")
        x_loaded = sem("x_loaded")
        proj_zeroed = sem("proj_zeroed")
        const_step = sem("const_step")
        const_ready = sem("const_ready")
        setup_step = sem("setup_step")
        setup_psum = sem("setup_psum")
        setup_copied = sem("setup_copied")
        search_step = sem("search_step")
        cnt_ready = sem("cnt_ready")
        tot_ready = sem("tot_ready")
        perturb_step = sem("perturb_step")
        weights_ready = sem("weights_ready")
        stats_step = sem("stats_step")
        stats_ready = sem("stats_ready")
        norm_step = sem("norm_step")
        rstd_ready = sem("rstd_ready")
        xn_ready = sem("xn_ready")
        xnT_psum = sem("xnT_psum")
        xnT_ready = sem("xnT_ready")
        ratio_step = sem("ratio_step")
        rstd2_ready = sem("rstd2_ready")
        logT_psum = sem("logT_psum")
        logT_ready = sem("logT_ready")
        z_psum = sem("z_psum")
        z_step = sem("z_step")
        z_ready = sem("z_ready")
        ez_ready = sem("ez_ready")
        prob_step = sem("prob_step")
        hid_psum = sem("hid_psum")
        hid_ready = sem("hid_ready")
        hid_used = sem("hid_used")
        y_ready = sem("y_ready")
        ytok_psum = sem("ytok_psum")
        y_added = sem("y_added")
        feat_psum = sem("feat_psum")
        feat_ready = sem("feat_ready")
        v_psum = sem("v_psum")
        v_ready = sem("v_ready")
        score_psum = sem("score_psum")
        aw_ready = sem("aw_ready")
        aw_used = sem("aw_used")
        ctxT_ready = sem("ctxT_ready")
        ctok_psum = sem("ctok_psum")
        norm_ctx_step = sem("norm_ctx_step")
        ctxn_ready = sem("ctxn_ready")
        ctxnT_psum = sem("ctxnT_psum")
        ctxnT_ready = sem("ctxnT_ready")
        attn_psum = sem("attn_psum")
        attn_added = sem("attn_added")
        bout_added = sem("bout_added")
        stored = sem("stored")

        N_W, N_COLS, N_X = 5, FC + 8 + H, 4
        XL = G // N_X

        block = ctx.enter_context(nc.Block())

        @block.sync
        def _(sp):
            sp.dma_start(w1[0][:, :, :], W1.rearrange("h (c f) -> h c f", c=FC)).then_inc(w_loaded, 16)
            sp.dma_start(w2[0][:, :, :], W2.rearrange("(c f) h -> f c h", c=FC)).then_inc(w_loaded, 16)
            sp.dma_start(wqkv_sb[:, :, :], Wqkv.rearrange("(a o) c -> o a c", a=3)).then_inc(w_loaded, 16)
            sp.dma_start(wout_sb[:, :], Wout).then_inc(w_loaded, 16)
            sp.dma_start(wr_sb[:, :], Wr).then_inc(w_loaded, 16)
            for n in range(N_X):
                sp.dma_start(x[:, n * XL:(n + 1) * XL, :], x_dram[:, n * XL:(n + 1) * XL, :]).then_inc(x_loaded, 16)
            with sp.Fori(0, NT) as i:
                sp.wait_ge(y_added, 2 * (i + NT) + 3)
                sp.dma_start(out_dram[:, bass.ds(i * SUB, SUB), :], x[:, bass.ds(i * SUB, SUB), :]).then_inc(stored, 16)
            sp.wait_ge(stored, 16 * NT)

        @block.scalar
        def _(act):
            for c in range(FC):
                act.dma_start(b1c[0][:, c:c + 1], b1[c * P:(c + 1) * P].rearrange("(f a) -> f a", a=1)).then_inc(cols_loaded, 16)
            act.dma_start(b2c[0][:, :], b2.rearrange("(h a) -> h a", a=1)).then_inc(cols_loaded, 16)
            for a in range(2):
                act.dma_start(bqk_sb[:, a:a + 1], bqkv[a * C:(a + 1) * C].rearrange("(o a) -> o a", a=1)).then_inc(cols_loaded, 16)
            act.dma_start(gamma_sb[:, :], gamma.rearrange("(h a) -> h a", a=1)).then_inc(cols_loaded, 16)
            act.dma_start(beta_sb[:, :], beta.rearrange("(h a) -> h a", a=1)).then_inc(cols_loaded, 16)
            act.dma_start(bv_rows[:, :], bqkv[2 * C:3 * C].rearrange("(a c) -> a c", a=1).to_broadcast([P, C])).then_inc(cols_loaded, 16)
            act.dma_start(bout_rows[:, :], bout.rearrange("(a c) -> a c", a=1).to_broadcast([P, C])).then_inc(cols_loaded, 16)
            act.dma_start(br_rows[:, :], br.rearrange("(a c) -> a c", a=1).to_broadcast([P, E])).then_inc(cols_loaded, 16)
            act.wait_ge(proj_zeroed, 1)
            for h in range(H):
                act.dma_start(proj_bd[h * D:(h + 1) * D, h * M:(h + 1) * M], proj[h]).then_inc(cols_loaded, 16)

            def xnT_copy(n):
                act.wait_ge(xnT_psum, n + 1)
                nc.scalar.copy(xnT[:, :], X_BANK[:, :]).then_inc(xnT_ready, 1)

            def ffn_body(t, n):
                for k in range(K2):
                    e, c = divmod(k, FC)
                    act.wait_ge(hid_psum, K2 * t + k + 1)
                    if k >= 4:
                        act.wait_ge(hid_used, K2 * t + k - 3)
                    nc.scalar.activation(hid[k % 4][:, :], H_BANK[k % 3][:, :], ACT.Gelu_apprx_tanh,
                                         bias=b1c[e][:, c:c + 1]).then_inc(hid_ready, 1)
                    if k == 1:
                        act.wait_ge(logT_psum, t + 1)
                        nc.scalar.copy(logT[:, :], L_BANK[:, 0:P]).then_inc(logT_ready, 1)
                    if k == 5:
                        act.wait_ge(hid_used, K2 * t + FC)
                        nc.scalar.activation(yT[0][:, :], Y_BANK[0][:, :], ACT.Identity,
                                             bias=b2c[0][:, 0:1]).then_inc(y_ready, 1)
                xnT_copy(n + 1)
                act.wait_ge(hid_used, K2 * (t + 1))
                nc.scalar.activation(yT[1][:, :], Y_BANK[1][:, :], ACT.Identity,
                                     bias=b2c[1][:, 0:1]).then_inc(y_ready, 1)

            def features(i, p):
                for a, (src, dst) in enumerate(((Q_BANK, qf), (KEY_BANK, kf))):
                    act.wait_ge(feat_psum, 2 * PAIRS * i + 2 * p + a + 1)
                    if p >= 2 and a == 0:
                        act.wait_ge(score_psum, COMBOS * i + 4 * (p - 1))
                    nc.scalar.activation(dst[p % 2][:, :], src[:, :], ACT.Relu,
                                         bias=feat_b[:, p, a:a + 1]).then_inc(feat_ready, 1)

            def ctx_copy(i, g):
                act.wait_ge(aw_used, COMBOS * i + 8 * (g + 1))
                nc.scalar.copy(ctxT[g % 2][:, :], C_BANK[:, :]).then_inc(ctxT_ready, 1)

            def attn_body(i, n):
                for p in range(PAIRS):
                    features(i, p)
                    if p >= 3 and p % 2 == 1:
                        ctx_copy(i, (p - 3) // 2)
                xnT_copy(n + 1)
                ctx_copy(i, GROUPS - 1)
                act.wait_ge(ctxnT_psum, i + 1)
                nc.scalar.copy(ctxnT[:, :], T_BANK[:, :]).then_inc(ctxnT_ready, 1)

            act.wait_ge(weights_ready, 1)
            xnT_copy(0)
            with act.Fori(0, NT) as i:
                ffn_body(i, i)
            with act.Fori(0, NT) as i:
                attn_body(i, i + NT)
            with act.Fori(0, NT) as i:
                ffn_body(i + NT, i + 2 * NT)

        @block.gpsimd
        def _(pool):
            nc.gpsimd.memset(proj_bd[:, :], 0.0).then_inc(proj_zeroed, 1)
            nc.gpsimd.memset(ident[:, :], 0.0).then_inc(const_step, 1)
            nc.gpsimd.memset(causal[:, :], 1.0).then_inc(const_step, 1)
            nc.gpsimd.memset(v_aug[:, :, :, :], 0.0).then_inc(const_step, 1)
            nc.gpsimd.memset(wr_g[:, :], 0.0).then_inc(const_step, 1)
            nc.gpsimd.memset(minus_half[:, :], -0.5).then_inc(const_step, 1)
            nc.gpsimd.memset(eps_tile[:, :], EPS).then_inc(const_step, 1)
            nc.gpsimd.memset(two[:, :, :], 2.0).then_inc(const_step, 1)
            nc.gpsimd.memset(ones16[:, :], 1.0).then_inc(const_step, 1)
            pool.wait_ge(const_step, 8)
            nc.gpsimd.affine_select(out=ident[:, :], in_=ident[:, :], compare_op=ALU.not_equal, fill=1.0,
                                    base=0, pattern=[[-1, P]], channel_multiplier=1).then_inc(const_step, 1)
            for lo in (0, S):
                nc.gpsimd.affine_select(out=causal[:, lo:lo + P], in_=causal[:, lo:lo + P], compare_op=ALU.is_ge,
                                        fill=0.0, base=0, pattern=[[1, P]],
                                        channel_multiplier=-1).then_inc(const_step, 1)
            nc.gpsimd.memset(v_aug[:, :, :, D:D + 1], 1.0).then_inc(const_step, 1)
            pool.wait_ge(const_step, 12)
            nc.gpsimd.memset(etot[:, :], 0.0).then_inc(const_ready, 1)
            nc.gpsimd.memset(erec[:, :], 0.0).then_inc(y_added, 1)

            def rstd_pow(n):
                pool.wait_ge(stats_ready, n + 1)
                step = Steps(pool, norm_step, 1 * n)
                step(nc.gpsimd.tensor_tensor(var_eps[:, :], mv[:, :, 1], eps_tile[:, :], ALU.add))
                nc.gpsimd.tensor_tensor(rstd[:, :], var_eps[:, :], minus_half[:, :], ALU.pow).then_inc(rstd_ready, 1)

            def ffn_body(t, n):
                pool.wait_ge(rstd_ready, n + 1)
                step = Steps(pool, ratio_step, 3 * t)
                step(nc.gpsimd.tensor_tensor(ratio[:, :], mv[:, :, 1], rstd[:, :], ALU.mult))
                step(nc.gpsimd.tensor_tensor(ratio[:, :], ratio[:, :], rstd[:, :], ALU.mult))
                step(nc.gpsimd.tensor_tensor(ratio[:, :], ratio[:, :], eps_tile[:, :], ALU.add))
                nc.gpsimd.tensor_tensor(rstd2[:, :], ratio[:, :], minus_half[:, :], ALU.pow).then_inc(rstd2_ready, 1)
                pool.wait_ge(z_ready, t + 1)
                nc.gpsimd.tensor_tensor(ez[:, :, :], two[:, :, :], z[:, :, :], ALU.pow).then_inc(ez_ready, 1)
                rstd_pow(n + 1)

            def attn_body(i, n):
                pool.wait_ge(xn_ready, n + 1)
                xt = x[:, bass.ds(i * SUB, SUB), :]
                nc.gpsimd.tensor_tensor(xt, xt, bout_rows[:, :].unsqueeze(1).to_broadcast([P, SUB, C]),
                                        ALU.add).then_inc(bout_added, 1)
                rstd_pow(n + 1)

            rstd_pow(0)
            pool.wait_ge(cols_loaded, 16 * N_COLS)
            with pool.Fori(0, NT) as i:
                ffn_body(i, i)
            with pool.Fori(0, NT) as i:
                attn_body(i, i + NT)
            with pool.Fori(0, NT) as i:
                ffn_body(i + NT, i + 2 * NT)

        @block.vector
        def _(dve):
            V = nc.vector
            setup = Steps(dve, setup_step, 0)

            def magnitude(dst, src):
                return V.tensor_scalar(dst.bitcast(I32), src.bitcast(I32), 0x7FFFFFFF, None, ALU.bitwise_and)

            dve.wait_ge(w_loaded, 16 * N_W)
            dve.wait_ge(cols_loaded, 16 * N_COLS)
            magnitude(a1[:, :], w1[0][:, :, :].rearrange("p c f -> p (c f)")).then_inc(setup_step, 1)
            magnitude(a2[:, :], w2[0][:, :, :].rearrange("p c f -> p (c f)")).then_inc(setup_step, 1)
            magnitude(ab1[:, :], b1c[0][:, :]).then_inc(setup_step, 1)
            magnitude(ab2[:, :], b2c[0][:, :]).then_inc(setup_step, 1)
            V.memset(found[:, :], 0).then_inc(setup_step, 1)
            V.memset(bit[:, :], 1 << 30).then_inc(setup_step, 1)
            setup.n = 6
            magnitudes = (a1, a2, ab1, ab2)
            for a, (n_w) in enumerate((C * FF, FF * C, FF, C)):
                k = max(1, int(n_w * SPARSITY / 2))
                V.memset(rank[:, 2 * a:2 * a + 1], float(k - 1)).then_inc(setup_step, 1)
                V.memset(rank[:, 2 * a + 1:2 * a + 2], float(n_w - k)).then_inc(setup_step, 1)
                setup.n += 2
            dve.wait_ge(const_ready, 1)
            V.tensor_scalar(wr_g[:, 0:E], wr_sb[:, :], gamma_sb[:, 0:1], LOG2E, ALU.mult, ALU.mult).then_inc(setup_step, 1)
            V.tensor_scalar(wr_l[:, :], wr_sb[:, :], LOG2E, None, ALU.mult).then_inc(setup_step, 1)
            setup.n += 2
            setup(V.tensor_copy(beta_wide[:, :], beta_sb[:, 0:1].to_broadcast([P, P])))
            dve.wait_ge(setup_psum, 1)
            V.tensor_copy(wv_t[:, :], bk[0][:, 0:P]).then_inc(setup_copied, 1)
            V.tensor_copy(wout_t[:, :], bk[0][:, P:2 * P]).then_inc(setup_copied, 1)
            V.tensor_copy(feat_b[:, :, :].rearrange("p a b -> p (a b)"), bk[1][:, 0:2 * PAIRS]).then_inc(setup_copied, 1)
            V.scalar_tensor_tensor(out=logit_b[:, :], in0=br_rows[:, :], scalar=LOG2E, in1=bk[1][:, 64:64 + E],
                                   op0=ALU.mult, op1=ALU.add).then_inc(setup_copied, 1)
            for a in range(2):
                for half in range(2):
                    V.tensor_copy(feat_w[:, a, half * 512:(half + 1) * 512],
                                  bk[2 + 2 * a + half][:, :]).then_inc(setup_copied, 1)

            with dve.Fori(0, 31) as b:
                step = Steps(dve, search_step, 5 * b)
                step(V.tensor_tensor(trial[:, :], found[:, :], bit[:, :], ALU.bitwise_or))
                for a, mag in enumerate(magnitudes):
                    for s in (2 * a, 2 * a + 1):
                        last = V.tensor_scalar(below[:, s, 0:mag.shape[1]], mag[:, :], trial[:, s:s + 1].bitcast(F32),
                                               None, ALU.is_lt, ALU.add, accum_out=cnt[:, s:s + 1])
                last.then_inc(cnt_ready, 1)
                dve.wait_ge(tot_ready, b + 1)
                step(V.tensor_tensor(keep[:, :], bk[0][:, 0:8], rank[:, :], ALU.is_le))
                step(V.tensor_tensor(keep[:, :], keep[:, :], bit[:, :], ALU.mult))
                step(V.tensor_tensor(found[:, :], found[:, :], keep[:, :], ALU.bitwise_or))
                step(V.tensor_scalar(bit[:, :], bit[:, :], 1, None, ALU.logical_shift_right))

            flat = "p c f -> p (c f)"
            step = Steps(dve, perturb_step, 0)
            for a, (mag, clean, pert) in enumerate((
                    (a1, w1[0][:, :, :].rearrange(flat), w1[1][:, :, :].rearrange(flat)),
                    (a2, w2[0][:, :, :].rearrange(flat), w2[1][:, :, :].rearrange(flat)),
                    (ab1, b1c[0][:, :], b1c[1][:, :]),
                    (ab2, b2c[0][:, :], b2c[1][:, :]))):
                w = mag.shape[1]
                top, bot = mask_top[:, 0:w], mask_bot[:, 0:w]
                step(V.tensor_scalar(top, mag[:, :], found[:, 2 * a + 1:2 * a + 2].bitcast(F32), None, ALU.is_ge))
                step(V.tensor_scalar(bot, mag[:, :], found[:, 2 * a:2 * a + 1].bitcast(F32), None, ALU.is_le))
                step(V.scalar_tensor_tensor(out=bot, in0=top, scalar=-2.0, in1=bot, op0=ALU.mult, op1=ALU.add))
                step(V.tensor_scalar(top, clean, SCALE, None, ALU.mult))
                step(V.scalar_tensor_tensor(out=bot, in0=bot, scalar=-1.0, in1=top, op0=ALU.max, op1=ALU.mult))
                step(V.tensor_tensor(pert, clean, bot, ALU.add))
            V.memset(etot[:, :], 0.0).then_inc(weights_ready, 1)

            def stats(n, tile):
                for g in range(SUB):
                    V.bn_stats(bn6[:, g, :], x[:, bass.ds(tile * SUB + g, 1), :]).then_inc(stats_step, 1)
                dve.wait_ge(stats_step, SUB * (n + 1))
                V.memset(spare[:, :], 0.0)
                for g in range(SUB):
                    last = V.bn_aggr(mv[:, g, :], bn6[:, g, :])
                last.then_inc(stats_ready, 1)

            def normalise(n, tile):
                dve.wait_ge(rstd_ready, n + 1)
                for g in range(SUB):
                    last = V.tensor_scalar(xn[:, g, :], x[:, bass.ds(tile * SUB + g, 1), :], mv[:, g, 0:1],
                                           rstd[:, g:g + 1], ALU.subtract, ALU.mult)
                last.then_inc(xn_ready, 1)

            def add_expert(t, e, tile):
                dve.wait_ge(ytok_psum, 2 * t + e + 1)
                for g in range(SUB):
                    xt = x[:, bass.ds(tile * SUB + g, 1), :]
                    last = V.scalar_tensor_tensor(out=xt, in0=YTOK_BANK[:, g * P:(g + 1) * P],
                                                  scalar=prob[:, e, g:g + 1], in1=xt, op0=ALU.mult, op1=ALU.add)
                last.then_inc(y_added, 1)

            def ffn_body(t, n, tile, following):
                dve.wait_ge(rstd2_ready, t + 1)
                dve.wait_ge(z_psum, t + 1)
                step = Steps(dve, z_step, 3 * t)
                raw = L_BANK[:, P:2 * P].rearrange("p (g w) -> p g w", g=SUB)[:, :, 0:E]
                step(V.tensor_tensor(z[:, :, :], raw, rstd2[:, :].unsqueeze(2).to_broadcast([P, SUB, E]), ALU.mult))
                step(V.tensor_tensor(z[:, :, :], z[:, :, :], logit_b[:, :].unsqueeze(1).to_broadcast([P, SUB, E]), ALU.add))
                step(V.tensor_reduce(zmax[:, :], z[:, :, :], AX_X, ALU.max))
                V.tensor_tensor(z[:, :, :], z[:, :, :], zmax[:, :].unsqueeze(2).to_broadcast([P, SUB, E]),
                                ALU.subtract).then_inc(z_ready, 1)
                stats(n + 1, following)
                dve.wait_ge(ez_ready, t + 1)
                step = Steps(dve, prob_step, 4 * t)
                step(V.tensor_reduce(esum[:, :], ez[:, :, 1:E], AX_X, ALU.add))
                step(V.tensor_tensor(etot[:, :], esum[:, :], ez[:, :, 0], ALU.add))
                step(V.reciprocal(erec[:, :], etot[:, :]))
                V.scalar_tensor_tensor(out=prob[:, 0, :], in0=ez[:, :, 0], scalar=0.5, in1=erec[:, :],
                                       op0=ALU.mult, op1=ALU.mult)
                step(V.scalar_tensor_tensor(out=prob[:, 1, :], in0=esum[:, :], scalar=0.5, in1=erec[:, :],
                                            op0=ALU.mult, op1=ALU.mult))
                add_expert(t, 0, tile)
                dve.wait_ge(xnT_psum, n + 1)
                normalise(n + 1, following)
                dve.wait_ge(y_added, 2 * t + 2)
                add_expert(t, 1, tile)

            def scores_masked(i, m):
                dve.wait_ge(score_psum, COMBOS * i + m + 1)
                if m >= 4:
                    dve.wait_ge(aw_used, COMBOS * i + m - 3)
                V.tensor_tensor(aw[m % 4][:, :], S_BANK[m % 3][:, 0:AW], causal[:, :], ALU.mult).then_inc(aw_ready, 1)

            def ctx_normalised(i, g):
                dve.wait_ge(ctok_psum, GROUPS * i + g + 1)
                raw = T_BANK[:, :].rearrange("p (s j w) -> p s j w", s=SUB, j=HG)
                step = Steps(dve, norm_ctx_step, 2 * (GROUPS * i + g))
                step(V.tensor_scalar(den[:, :, :], raw[:, :, :, D], DELTA, None, ALU.add))
                step(V.reciprocal(rden[:, :, :], den[:, :, :]))
                part = ctxn[:, :, g * HG * D:(g + 1) * HG * D].rearrange("p s (j d) -> p s j d", j=HG)
                V.tensor_tensor(part, raw[:, :, :, 0:D], rden[:, :, :].unsqueeze(3).to_broadcast([P, SUB, HG, D]),
                                ALU.mult).then_inc(ctxn_ready, 1)

            def attn_body(i, n, tile, following):
                dve.wait_ge(v_psum, i + 1)
                V.tensor_tensor(v_aug[:, :, :, 0:D], X_BANK[:, :].rearrange("p (s h d) -> p s h d", s=SUB, h=H),
                                bv_rows[:, :].rearrange("p (h d) -> p h d", h=H).unsqueeze(1).to_broadcast([P, SUB, H, D]),
                                ALU.add).then_inc(v_ready, 1)
                for m in range(COMBOS):
                    scores_masked(i, m)
                    if m >= 13 and m % 8 == 5:
                        ctx_normalised(i, (m - 13) // 8)
                    if m == 8:
                        stats(n + 1, following)
                    if m == 24:
                        dve.wait_ge(xnT_psum, n + 1)
                        normalise(n + 1, following)
                ctx_normalised(i, GROUPS - 1)
                dve.wait_ge(attn_psum, i + 1)
                dve.wait_ge(bout_added, i + 1)
                xt = x[:, bass.ds(tile * SUB, SUB), :]
                V.tensor_tensor(xt, C_BANK[:, :].rearrange("p (s c) -> p s c", s=SUB), xt, ALU.add).then_inc(attn_added, 1)

            dve.wait_ge(x_loaded, 16 * N_X)
            stats(0, 0)
            normalise(0, 0)
            with dve.Fori(0, NT) as i:
                ffn_body(i, i, i, (i + 1) % NT)
            with dve.Fori(0, NT) as i:
                attn_body(i, i + NT, i, (i + 1) % NT)
            with dve.Fori(0, NT) as i:
                ffn_body(i + NT, i + 2 * NT, i, (i + 1) % NT)

        @block.tensor
        def _(pe):
            mm = nc.tensor.matmul
            pe.wait_ge(const_ready, 1)
            pe.wait_ge(w_loaded, 16 * N_W)
            pe.wait_ge(cols_loaded, 16 * N_COLS)
            nc.tensor.transpose(bk[0][:, 0:P], wqkv_sb[:, 2, :], ident[:, :])
            nc.tensor.transpose(bk[0][:, P:2 * P], wout_sb[:, :], ident[:, :])
            for a in range(2):
                for half in range(2):
                    mm(bk[2 + 2 * a + half][:, :], wqkv_sb[:, a, :], proj_bd[:, half * 512:(half + 1) * 512],
                       start=True, stop=True)
            for p in range(PAIRS):
                mm(bk[1][:, 2 * p:2 * p + 2], proj_bd[:, p * P:(p + 1) * P], bqk_sb[:, :], start=True, stop=True)
            pe.wait_ge(setup_step, 17)
            mm(bk[1][:, 64:64 + E], beta_wide[:, :], wr_l[:, :], start=True, stop=True).then_inc(setup_psum, 1)
            pe.wait_ge(setup_copied, 8)
            with pe.Fori(0, 31) as b:
                pe.wait_ge(cnt_ready, b + 1)
                mm(bk[0][:, 0:8], ones16[:, :], cnt[:, :], start=True, stop=True).then_inc(tot_ready, 1)

            def xn_transposed(n):
                pe.wait_ge(xn_ready, n + 1)
                for g in range(SUB):
                    last = nc.tensor.transpose(X_BANK[:, g * P:(g + 1) * P], xn[:, g, :], ident[:, :])
                last.then_inc(xnT_psum, 1)

            def ffn_body(t, n):
                def hidden(k):
                    e, c = divmod(k, FC)
                    if k >= 3:
                        pe.wait_ge(hid_ready, K2 * t + k - 2)
                    mm(H_BANK[k % 3][:, :], w1[e][:, c, :], xnT[:, :], start=True, stop=True).then_inc(hid_psum, 1)

                def output(k):
                    e, c = divmod(k, FC)
                    pe.wait_ge(hid_ready, K2 * t + k + 1)
                    last = mm(Y_BANK[e][:, :], w2[e][:, c, :], hid[k % 4][:, :], start=(c == 0), stop=(c == FC - 1))
                    last.then_inc(hid_used, 1)

                def y_transposed(e):
                    pe.wait_ge(y_ready, 2 * t + e + 1)
                    pe.wait_ge(y_added, 2 * t + e + 1)
                    for g in range(SUB):
                        last = nc.tensor.transpose(YTOK_BANK[:, g * P:(g + 1) * P], yT[e][:, g * P:(g + 1) * P],
                                                   ident[:, :])
                    last.then_inc(ytok_psum, 1)

                pe.wait_ge(xnT_ready, n + 1)
                hidden(0)
                hidden(1)
                for g in range(SUB):
                    last = mm(L_BANK[g * VW:(g + 1) * VW, 0:P], wr_g[:, :], xnT[:, g * P:(g + 1) * P],
                              start=True, stop=True, tile_position=(0, g * VW))
                last.then_inc(logT_psum, 1)
                hidden(2)
                output(0)
                pe.wait_ge(logT_ready, t + 1)
                nc.tensor.transpose(L_BANK[:, P:2 * P], logT[:, :], ident[:, :]).then_inc(z_psum, 1)
                for k in range(3, K2):
                    hidden(k)
                    output(k - 2)
                    if k == 6:
                        y_transposed(0)
                output(6)
                output(7)
                xn_transposed(n + 1)
                y_transposed(1)

            def attn_body(i, n):
                def features(p):
                    if p >= 1:
                        pe.wait_ge(feat_ready, 2 * (PAIRS * i + p))
                    for a, dst in enumerate((Q_BANK, KEY_BANK)):
                        mm(dst[:, :], feat_w[:, a, p * P:(p + 1) * P], xnT[:, :], start=True,
                           stop=True).then_inc(feat_psum, 1)

                def scores(m):
                    p, b, e = m // 4, m // 2 % 2, m % 2
                    rows = slice(e * M, (e + 1) * M)
                    if m % 4 == 0:
                        pe.wait_ge(feat_ready, 2 * (PAIRS * i + p + 1))
                    if m >= 3:
                        pe.wait_ge(aw_ready, COMBOS * i + m - 2)
                    q, k, o = qf[p % 2], kf[p % 2], S_BANK[m % 3]
                    mm(o[:, 0:S], k[rows, b * S:b * S + P], q[rows, b * S:(b + 1) * S], start=True, stop=True)
                    mm(o[:, S:AW], k[rows, b * S + P:(b + 1) * S], q[rows, b * S + P:(b + 1) * S],
                       start=True, stop=True).then_inc(score_psum, 1)

                def context(m):
                    p, b, e = m // 4, m // 2 % 2, m % 2
                    g, j = divmod(2 * p + e, HG)
                    if m == 0:
                        pe.wait_ge(v_ready, i + 1)
                    if m % 8 == 0 and m > 0:
                        pe.wait_ge(ctxT_ready, GROUPS * i + g)
                    pe.wait_ge(aw_ready, COMBOS * i + m + 1)
                    rows = slice(j * VW, (j + 1) * VW)
                    h = 2 * p + e
                    mm(C_BANK[rows, b * S:(b + 1) * S], v_aug[:, 2 * b, h, :], aw[m % 4][:, 0:S], start=True,
                       stop=False, tile_position=(0, j * VW))
                    last = mm(C_BANK[rows, b * S + P:(b + 1) * S], v_aug[:, 2 * b + 1, h, :], aw[m % 4][:, S:AW],
                              start=False, stop=True, tile_position=(0, j * VW))
                    last.then_inc(aw_used, 1)

                def ctx_transposed(g):
                    pe.wait_ge(ctxT_ready, GROUPS * i + g + 1)
                    if g >= 1:
                        pe.wait_ge(ctxn_ready, GROUPS * i + g)
                    for s in range(SUB):
                        last = nc.tensor.transpose(T_BANK[:, s * P:(s + 1) * P], ctxT[g % 2][:, s * P:(s + 1) * P],
                                                   ident[:, :])
                    last.then_inc(ctok_psum, 1)

                pe.wait_ge(xnT_ready, n + 1)
                features(0)
                for s in range(SUB):
                    last = mm(X_BANK[:, s * P:(s + 1) * P], xnT[:, s * P:(s + 1) * P], wv_t[:, :], start=True, stop=True)
                last.then_inc(v_psum, 1)
                for m in range(COMBOS):
                    if m % 4 == 0 and m // 4 + 1 < PAIRS:
                        features(m // 4 + 1)
                    scores(m)
                    if m >= 2:
                        context(m - 2)
                    if m >= 12 and m % 8 == 4:
                        ctx_transposed((m - 12) // 8)
                    if m == 30:
                        xn_transposed(n + 1)
                context(COMBOS - 2)
                context(COMBOS - 1)
                ctx_transposed(GROUPS - 1)
                pe.wait_ge(ctxn_ready, GROUPS * (i + 1))
                for s in range(SUB):
                    last = nc.tensor.transpose(T_BANK[:, s * P:(s + 1) * P], ctxn[:, s, :], ident[:, :])
                last.then_inc(ctxnT_psum, 1)
                pe.wait_ge(ctxnT_ready, i + 1)
                for s in range(SUB):
                    last = mm(C_BANK[:, s * P:(s + 1) * P], ctxnT[:, s * P:(s + 1) * P], wout_t[:, :],
                              start=True, stop=True)
                last.then_inc(attn_psum, 1)

            pe.wait_ge(weights_ready, 1)
            xn_transposed(0)
            with pe.Fori(0, NT) as i:
                ffn_body(i, i)
            with pe.Fori(0, NT) as i:
                attn_body(i, i + NT)
            pe.wait_ge(attn_added, NT)
            with pe.Fori(0, NT) as i:
                ffn_body(i + NT, i + 2 * NT)


_INS = ["L0_attn_x", "L0_attn_Wqkv", "L0_attn_bqkv", "L0_attn_Wout", "L0_attn_bout", "L0_attn_proj", "L0_ffn_W1",
        "L0_ffn_b1", "L0_ffn_W2", "L0_ffn_b2", "L0_ffn_ln_gamma", "L0_ffn_ln_beta", "L0_ffn_Wr", "L0_ffn_br"]


def kernel(**inputs):
    import numpy as np
    import concourse.bacc as bacc
    from concourse.bass_utils import run_bass_kernel_spmd

    nc = bacc.Bacc("TRN2", target_bir_lowering=False, num_devices=1)
    arrays, args = {}, []
    for name in _INS:
        a = np.ascontiguousarray(inputs[name])
        arrays["in_" + name] = a
        args.append(nc.dram_tensor("in_" + name, a.shape, mybir.dt.from_np(a.dtype), kind="ExternalInput").ap())
    shape = arrays["in_L0_attn_x"].shape
    out = nc.dram_tensor("out_x", shape, F32, kind="ExternalOutput").ap()
    macaron_kernel(nc, *args, out)
    r = run_bass_kernel_spmd(nc, [arrays], core_ids=[0])
    return r.results[0]["out_x"]
```

```python
import math
from contextlib import ExitStack

import concourse.bass as bass
from concourse import mybir

F32 = mybir.dt.float32
F16 = mybir.dt.float16
F32R = mybir.dt.float32r
I32 = mybir.dt.int32
ALU = mybir.AluOpType
ACT = mybir.ActivationFunctionType
AX_X = mybir.AxisListType.X

P = 128
EPS = 1e-5
DELTA = 1e-6
LOG2E = math.log2(math.e)
SCALE, SPARSITY = 0.8, 0.1


class Steps:

    def __init__(self, eng, sem, before):
        self.eng, self.sem, self.before, self.n = eng, sem, before, 0

    def __call__(self, ins):
        self.n += 1
        ins.then_inc(self.sem, 1)
        self.eng.wait_ge(self.sem, self.before + self.n)


def macaron_kernel(nc, x_in, Wqkv, bqkv, Wout, bout, proj, W1, b1, W2, b2, gamma, beta, Wr, br, out):
    B, S, C = x_in.shape
    H, D, M = proj.shape
    FF = W1.shape[1]
    E = Wr.shape[1]
    G = B * S // P
    SUB = 4
    T = SUB * P
    NT = G // SUB
    NSEQ = T // S
    FC = FF // P
    K2 = 2 * FC
    PAIRS = H // 2
    COMBOS = NSEQ * H
    HG = 4
    GROUPS = H // HG
    COPIES = P // (HG * D)
    VW = 32
    AW = S + P
    assert C == P and H * D == P and S == 2 * P and 2 * M == P and NSEQ == 2 and FC == 4

    x_dram = x_in.rearrange("b (g p) c -> p (b g) c", p=P)
    out_dram = out.rearrange("b (g p) c -> p (b g) c", p=P)

    with ExitStack() as ctx:
        def sb(name, shape, dt=F32):
            return ctx.enter_context(nc.sbuf_tensor(name, shape, dt))

        def bank(name):
            return ctx.enter_context(nc.psum_tensor(name, [P, 512], F32))

        def sem(name):
            return ctx.enter_context(nc.semaphore(name))

        x = sb("x_all", [P, G, C])
        ident = sb("ident", [P, P])
        causal = sb("causal", [P, AW])
        w1 = [sb("w1_clean", [P, FC, P]), sb("w1_perturbed", [P, FC, P])]
        w2 = [sb("w2_clean", [P, FC, P]), sb("w2_perturbed", [P, FC, P])]
        b1c = [sb("b1_clean", [P, FC]), sb("b1_perturbed", [P, FC])]
        b2c = [sb("b2_clean", [P, 1]), sb("b2_perturbed", [P, 1])]
        wqkv_sb = sb("wqkv_sb", [P, 3, C])
        wout_sb = sb("wout_sb", [P, C])
        bqk_sb = sb("bqk_sb", [P, 2])
        proj_copies = sb("proj_copies", [P, H * M])
        wr_sb = sb("wr_sb", [P, E])
        gamma_sb = sb("gamma_sb", [P, 1])
        beta_sb = sb("beta_sb", [P, 1])
        bv_rows = sb("bv_rows", [P, C])
        bout_rows = sb("bout_rows", [P, C])
        br_rows = sb("br_rows", [P, E])
        wv_t = sb("wv_t", [P, C])
        wout_t = sb("wout_t", [P, C])
        wqk_t = sb("wqk_t", [P, 2, C])
        wqk_h = sb("wqk_h", [P, 2, C], F32R)
        wqk_l = sb("wqk_l", [P, 2, C], F32R)
        proj_parts = sb("proj_parts", [P, H * M], F32R)
        w1h = [sb("w1h_clean", [P, FC, P], F32R), sb("w1h_perturbed", [P, FC, P], F32R)]
        w1l = [sb("w1l_clean", [P, FC, P], F32R), sb("w1l_perturbed", [P, FC, P], F32R)]
        wr_g = sb("wr_g", [P, VW])
        beta_wide = sb("beta_wide", [P, P])
        wr_l = sb("wr_l", [P, E])
        logit_b = sb("logit_b", [P, E])
        BITS = 31
        mag = [sb("abs_w1", [P, FF]), sb("abs_w2", [P, FF])]
        ab1 = sb("abs_b1", [P, FC])
        ab2 = sb("abs_b2", [P, 1])
        ab1_row = sb("abs_b1_row", [P, FF])
        ab2_row = sb("abs_b2_row", [P, C])
        below = [sb(f"below{g}", [P, 2, FF], F16) for g in range(2)]
        mask_top = sb("mask_top", [P, FF])
        mask_bot = sb("mask_bot", [P, FF])
        junk = sb("junk", [P, FF])
        ones16 = sb("ones16", [P, P], F16)
        found = [sb(f"found{g}", [P, 2], I32) for g in range(2)]
        trial = [sb(f"trial{g}", [P, 2], I32) for g in range(2)]
        keep = [sb(f"keep{g}", [P, 2], I32) for g in range(2)]
        cnt = [sb(f"cnt{g}", [P, 2], F16) for g in range(2)]
        bits = sb("bits", [P, BITS], I32)
        bits_f = sb("bits_f", [P, BITS])
        n_less = sb("n_less", [P, FC + 1])
        n_more = sb("n_more", [P, FC + 1])
        bn6 = sb("bn6", [P, SUB, 6])
        mv = sb("mean_var", [P, SUB, 2])
        minus_half = sb("minus_half", [P, SUB])
        var_eps = sb("var_eps", [P, SUB])
        eps_tile = sb("eps_tile", [P, SUB])
        spare = sb("spare", [P, 1])
        gelu_warm = sb("gelu_warm", [P, 1])
        rstd = sb("rstd", [P, SUB])
        ratio = sb("ratio", [P, SUB])
        rstd2 = sb("rstd2", [P, SUB])
        xn = sb("xn", [P, SUB, C])
        xnT = sb("xnT", [P, T])
        xnTh = sb("xnTh", [P, T], F32R)
        xnTl = sb("xnTl", [P, T], F32R)
        two = sb("two", [P, SUB, E])
        logT = sb("logT", [P, P])
        z = sb("z", [P, SUB, E])
        zmax = sb("zmax", [P, SUB])
        ez = sb("ez", [P, SUB, E])
        esum = sb("esum", [P, SUB])
        etot = sb("etot", [P, SUB])
        erec = sb("erec", [P, SUB])
        prob = sb("prob", [P, 2, SUB])
        hid = [sb(f"hid{i}", [P, T]) for i in range(4)]
        yT = [sb(f"yT{i}", [P, T]) for i in range(2)]
        qk_part = [sb("qk_high", [P, 2, T], F32R), sb("qk_low", [P, 2, T], F32R)]
        qk_stack = sb("qk_stack", [P, 2, GROUPS, T], F32R)
        qf = [sb(f"qf{i}", [P, T]) for i in range(2)]
        kf = [sb(f"kf{i}", [P, T]) for i in range(2)]
        v_aug = sb("v_aug", [P, SUB, H, VW])
        aw = [sb(f"aw{i}", [P, AW]) for i in range(4)]
        ctxT = [sb(f"ctxT{i}", [P, T]) for i in range(2)]
        den = sb("den", [P, SUB, HG])
        rden = sb("rden", [P, SUB, HG])
        ctxn = sb("ctxn", [P, SUB, C])
        ctxnT = sb("ctxnT", [P, T])

        bk = [bank(f"bank{i}") for i in range(8)]
        X_BANK = bk[7]
        CNT_BANK = [bk[4], bk[5]]
        TOT_BANK = [bk[6], bk[7]]
        H_BANK = [bk[0], bk[1], bk[2]]
        Y_BANK = [bk[3], bk[4]]
        YTOK_BANK = bk[5]
        L_BANK = bk[6]
        Q_BANK, KEY_BANK = bk[0], bk[1]
        S_BANK = [bk[2], bk[3], bk[4]]
        C_BANK = bk[5]
        T_BANK = bk[6]

        w1_loaded = sem("w1_loaded")
        w2_loaded = sem("w2_loaded")
        w_loaded = sem("w_loaded")
        cols_loaded = sem("cols_loaded")
        x0_loaded = sem("x0_loaded")
        x_loaded = sem("x_loaded")
        proj_zeroed = sem("proj_zeroed")
        const_step = sem("const_step")
        const_ready = sem("const_ready")
        setup_step = sem("setup_step")
        setup_psum = sem("setup_psum")
        setup_copied = sem("setup_copied")
        search_step = sem("search_step")
        mask_ready = sem("mask_ready")
        cnt_psum = sem("cnt_psum")
        cnt_ready = sem("cnt_ready")
        tot_ready = sem("tot_ready")
        b_loaded = sem("b_loaded")
        bits_ready = sem("bits_ready")
        logit_b_psum = sem("logit_b_psum")
        logit_b_copied = sem("logit_b_copied")
        perturb_step = sem("perturb_step")
        weights_ready = sem("weights_ready")
        stats_step = sem("stats_step")
        stats_ready = sem("stats_ready")
        norm_step = sem("norm_step")
        rstd_ready = sem("rstd_ready")
        xn_ready = sem("xn_ready")
        xnT_psum = sem("xnT_psum")
        xnT_ready = sem("xnT_ready")
        xnTh_step = sem("xnTh_step")
        xnT_split = sem("xnT_split")
        w1h_ready = sem("w1h_ready")
        w1h_p_ready = sem("w1h_p_ready")
        clean_ready = sem("clean_ready")
        proj_rounded = sem("proj_rounded")
        feat_w_ready = sem("feat_w_ready")
        b_ready = sem("b_ready")
        ratio_step = sem("ratio_step")
        rstd2_ready = sem("rstd2_ready")
        logT_psum = sem("logT_psum")
        logT_ready = sem("logT_ready")
        z_psum = sem("z_psum")
        z_step = sem("z_step")
        z_ready = sem("z_ready")
        ez_ready = sem("ez_ready")
        prob_step = sem("prob_step")
        hid_psum = sem("hid_psum")
        hid_ready = sem("hid_ready")
        hid_used = sem("hid_used")
        y_ready = sem("y_ready")
        ytok_psum = sem("ytok_psum")
        y_added = sem("y_added")
        qk_psum = sem("qk_psum")
        qk_high_ready = sem("qk_high_ready")
        qk_low_ready = sem("qk_low_ready")
        stacked = [sem(f"stacked{g}") for g in range(GROUPS)]
        feat_psum = sem("feat_psum")
        feat_ready = sem("feat_ready")
        v_psum = sem("v_psum")
        v_ready = sem("v_ready")
        score_psum = sem("score_psum")
        aw_ready = sem("aw_ready")
        aw_used = sem("aw_used")
        ctxT_ready = sem("ctxT_ready")
        ctok_psum = sem("ctok_psum")
        norm_ctx_step = sem("norm_ctx_step")
        ctxn_ready = sem("ctxn_ready")
        ctxnT_psum = sem("ctxnT_psum")
        ctxnT_ready = sem("ctxnT_ready")
        attn_psum = sem("attn_psum")
        attn_added = sem("attn_added")
        bout_added = sem("bout_added")
        stored = sem("stored")

        N_W, N_COLS, N_B, N_X = 3, 7 + COPIES * HG, FC + 3, 5
        XL = (G - SUB) // N_X

        block = ctx.enter_context(nc.Block())

        @block.sync
        def _(sp):
            sp.dma_start(w1[0][:, :, :], W1.rearrange("h (c f) -> h c f", c=FC)).then_inc(w1_loaded, 16)
            sp.dma_start(w2[0][:, :, :], W2.rearrange("(c f) h -> f c h", c=FC)).then_inc(w2_loaded, 16)
            sp.dma_start(wqkv_sb[:, :, :], Wqkv.rearrange("(a o) c -> o a c", a=3)).then_inc(w_loaded, 16)
            sp.dma_start(wout_sb[:, :], Wout).then_inc(w_loaded, 16)
            sp.dma_start(wr_sb[:, :], Wr).then_inc(w_loaded, 16)
            sp.dma_start(x[:, 0:SUB, :], x_dram[:, 0:SUB, :]).then_inc(x0_loaded, 16)
            sp.wait_ge(proj_zeroed, 1)
            for c in range(COPIES):
                for j in range(HG):
                    lo = c * HG * D + j * D
                    sp.dma_start(proj_copies[lo:lo + D, :].rearrange("d (g j m) -> d g j m", j=HG, m=M)[:, :, j, :],
                                 proj.rearrange("(g j) d m -> d g j m", j=HG)[:, :, j, :]).then_inc(cols_loaded, 16)
            for lo in range(SUB, G, XL):
                sp.dma_start(x[:, lo:lo + XL, :], x_dram[:, lo:lo + XL, :]).then_inc(x_loaded, 16)


            def stack(i, first):
                sp.wait_ge(qk_low_ready, 2 * (i + 1))
                for g in range(GROUPS):
                    if not first:
                        sp.wait_ge(feat_psum, 2 * PAIRS * (i - 1) + 4 * (g + 1))
                    for c in range(COPIES):
                        sp.dma_start(qk_stack[c * HG * D:(c + 1) * HG * D, :, g, :].bitcast(F32),
                                     qk_part[c % 2][g * HG * D:(g + 1) * HG * D, :, :].bitcast(F32)).then_inc(stacked[g], 16)

            stack(0, True)
            with sp.Fori(1, NT) as i:
                stack(i, False)
            with sp.Fori(0, NT) as i:
                sp.wait_ge(y_added, 2 * (i + NT) + 3)
                sp.dma_start(out_dram[:, bass.ds(i * SUB, SUB), :], x[:, bass.ds(i * SUB, SUB), :]).then_inc(stored, 16)
            sp.wait_ge(stored, 16 * NT)

        @block.scalar
        def _(act):
            column = lambda v: v.rearrange("(f a) -> f a", a=1)
            row = lambda v, n: v.rearrange("(a c) -> a c", a=1).to_broadcast([P, n])
            for c in range(FC):
                act.dma_start(b1c[0][:, c:c + 1], column(b1[c * P:(c + 1) * P])).then_inc(b_loaded, 16)
            act.dma_start(b2c[0][:, :], column(b2)).then_inc(b_loaded, 16)
            act.dma_start(ab1_row[:, :], row(b1, FF)).then_inc(b_loaded, 16)
            act.dma_start(ab2_row[:, :], row(b2, C)).then_inc(b_loaded, 16)
            for a in range(2):
                act.dma_start(bqk_sb[:, a:a + 1], column(bqkv[a * C:(a + 1) * C])).then_inc(cols_loaded, 16)
            act.dma_start(gamma_sb[:, :], column(gamma)).then_inc(cols_loaded, 16)
            act.dma_start(beta_sb[:, :], column(beta)).then_inc(cols_loaded, 16)
            act.dma_start(bv_rows[:, :], row(bqkv[2 * C:3 * C], C)).then_inc(cols_loaded, 16)
            act.dma_start(bout_rows[:, :], row(bout, C)).then_inc(cols_loaded, 16)
            act.dma_start(br_rows[:, :], row(br, E)).then_inc(cols_loaded, 16)

            def xnT_copy(n):
                act.wait_ge(xnT_psum, n + 1)
                nc.scalar.copy(xnT[:, :], X_BANK[:, :]).then_inc(xnT_ready, 1)

            def ffn_body(t, n):
                for k in range(K2):
                    e, c = divmod(k, FC)
                    if k == FC and isinstance(t, int) and t == 0:
                        act.wait_ge(b_ready, 1)
                    if k == 6:
                        xnT_copy(n + 1)
                    act.wait_ge(hid_psum, K2 * t + k + 1)
                    if k >= 4:
                        act.wait_ge(hid_used, K2 * t + k - 3)
                    nc.scalar.activation(hid[k % 4][:, :], H_BANK[k % 3][:, :], ACT.Gelu_apprx_tanh,
                                         bias=b1c[e][:, c:c + 1]).then_inc(hid_ready, 1)
                    if k == 1:
                        act.wait_ge(logT_psum, t + 1)
                        nc.scalar.copy(logT[:, :], L_BANK[:, 0:P]).then_inc(logT_ready, 1)
                    if k == 5:
                        act.wait_ge(hid_used, K2 * t + FC)
                        nc.scalar.activation(yT[0][:, :], Y_BANK[0][:, :], ACT.Identity,
                                             bias=b2c[0][:, 0:1]).then_inc(y_ready, 1)
                act.wait_ge(hid_used, K2 * (t + 1))
                nc.scalar.activation(yT[1][:, :], Y_BANK[1][:, :], ACT.Identity,
                                     bias=b2c[1][:, 0:1]).then_inc(y_ready, 1)

            def features(i, p):
                for a, (src, dst) in enumerate(((Q_BANK, qf), (KEY_BANK, kf))):
                    act.wait_ge(feat_psum, 2 * PAIRS * i + 2 * p + a + 1)
                    if p >= 2 and a == 0:
                        act.wait_ge(score_psum, COMBOS * i + 4 * (p - 1))
                    nc.scalar.activation(dst[p % 2][:, :], src[:, :], ACT.Relu).then_inc(feat_ready, 1)

            def qk_high(i, a):
                act.wait_ge(qk_psum, 2 * i + a + 1)
                if not (isinstance(i, int) and i == 0):
                    for g in range(GROUPS):
                        act.wait_ge(stacked[g], 16 * COPIES * i)
                nc.scalar.activation(qk_part[0][:, a, :], X_BANK[:, :], ACT.Identity,
                                     bias=bqk_sb[:, a:a + 1]).then_inc(qk_high_ready, 1)

            def ctx_copy(i, g):
                act.wait_ge(aw_used, COMBOS * i + 8 * (g + 1))
                nc.scalar.copy(ctxT[g % 2][:, :], C_BANK[:, :]).then_inc(ctxT_ready, 1)

            def ctxn_copy(i):
                act.wait_ge(ctxnT_psum, i + 1)
                nc.scalar.copy(ctxnT[:, :], T_BANK[:, :]).then_inc(ctxnT_ready, 1)

            def attn_body(i, n, first):
                for p in range(PAIRS):
                    features(i, p)
                    if p == 2 and not first:
                        ctxn_copy(i - 1)
                    if p >= 3 and p % 2 == 1:
                        ctx_copy(i, (p - 3) // 2)
                    if p == 4:
                        xnT_copy(n + 1)
                    if p in (5, 6):
                        qk_high(i + 1, p - 5)
                ctx_copy(i, GROUPS - 1)

            act.wait_ge(b_loaded, 16 * N_B)
            nc.scalar.activation(gelu_warm[:, :], b2c[0][:, :], ACT.Gelu_apprx_tanh)
            with act.Fori(0, BITS) as b:
                for g in range(2):
                    act.wait_ge(cnt_psum, 2 * b + g + 1)
                    nc.scalar.copy(cnt[g][:, :], CNT_BANK[g][:, 0:2]).then_inc(cnt_ready, 1)
            xnT_copy(0)
            act.wait_ge(setup_psum, 1)
            nc.scalar.copy(wv_t[:, :], bk[0][:, 0:P]).then_inc(setup_copied, 1)
            nc.scalar.copy(wout_t[:, :], bk[0][:, P:2 * P]).then_inc(setup_copied, 1)
            qk_cols = bk[0][:, 2 * P:4 * P].rearrange("p (a o) -> p a o", a=2)
            nc.scalar.copy(wqk_h[:, :, :], qk_cols).then_inc(setup_copied, 1)
            nc.scalar.copy(wqk_t[:, :, :], qk_cols).then_inc(setup_copied, 1)
            ffn_body(0, 0)
            with act.Fori(1, NT) as i:
                ffn_body(i, i)
            act.wait_ge(cols_loaded, 16 * N_COLS)
            qk_high(0, 0)
            qk_high(0, 1)
            attn_body(0, NT, True)
            with act.Fori(1, NT) as i:
                attn_body(i, i + NT, False)
            ctxn_copy(NT - 1)
            with act.Fori(0, NT) as i:
                ffn_body(i + NT, i + 2 * NT)

        @block.gpsimd
        def _(pool):
            nc.gpsimd.memset(proj_copies[:, :], 0.0).then_inc(proj_zeroed, 1)
            nc.gpsimd.memset(ident[:, :], 0.0).then_inc(const_step, 1)
            nc.gpsimd.memset(causal[:, :], 1.0).then_inc(const_step, 1)
            nc.gpsimd.memset(v_aug[:, :, :, :], 0.0).then_inc(const_step, 1)
            nc.gpsimd.memset(wr_g[:, :], 0.0).then_inc(const_step, 1)
            nc.gpsimd.memset(minus_half[:, :], -0.5).then_inc(const_step, 1)
            nc.gpsimd.memset(eps_tile[:, :], EPS).then_inc(const_step, 1)
            nc.gpsimd.memset(two[:, :, :], 2.0).then_inc(const_step, 1)
            nc.gpsimd.memset(ones16[:, :], 1.0).then_inc(const_step, 1)
            pool.wait_ge(const_step, 8)
            nc.gpsimd.affine_select(out=ident[:, :], in_=ident[:, :], compare_op=ALU.not_equal, fill=1.0,
                                    base=0, pattern=[[-1, P]], channel_multiplier=1).then_inc(const_step, 1)
            for lo in (0, S):
                nc.gpsimd.affine_select(out=causal[:, lo:lo + P], in_=causal[:, lo:lo + P], compare_op=ALU.is_ge,
                                        fill=0.0, base=0, pattern=[[1, P]],
                                        channel_multiplier=-1).then_inc(const_step, 1)
            nc.gpsimd.memset(v_aug[:, :, :, D:D + 1], 1.0).then_inc(const_step, 1)
            pool.wait_ge(const_step, 12)
            nc.gpsimd.memset(etot[:, :], 0.0).then_inc(const_ready, 1)
            nc.gpsimd.memset(erec[:, :], 0.0).then_inc(y_added, 1)

            for b in range(BITS):
                nc.gpsimd.memset(bits[:, b:b + 1], 1 << (BITS - 1 - b))
                last = nc.gpsimd.memset(bits_f[:, b:b + 1], float(1 << (BITS - 1 - b)))
            last.then_inc(bits_ready, 1)

            def rstd_pow(n):
                pool.wait_ge(stats_ready, n + 1)
                step = Steps(pool, norm_step, 1 * n)
                step(nc.gpsimd.tensor_tensor(var_eps[:, :], mv[:, :, 1], eps_tile[:, :], ALU.add))
                nc.gpsimd.tensor_tensor(rstd[:, :], var_eps[:, :], minus_half[:, :], ALU.pow).then_inc(rstd_ready, 1)

            def ffn_body(t, n):
                pool.wait_ge(rstd_ready, n + 1)
                step = Steps(pool, ratio_step, 3 * t)
                step(nc.gpsimd.tensor_tensor(ratio[:, :], mv[:, :, 1], rstd[:, :], ALU.mult))
                step(nc.gpsimd.tensor_tensor(ratio[:, :], ratio[:, :], rstd[:, :], ALU.mult))
                step(nc.gpsimd.tensor_tensor(ratio[:, :], ratio[:, :], eps_tile[:, :], ALU.add))
                nc.gpsimd.tensor_tensor(rstd2[:, :], ratio[:, :], minus_half[:, :], ALU.pow).then_inc(rstd2_ready, 1)
                rstd_pow(n + 1)
                pool.wait_ge(z_ready, t + 1)
                nc.gpsimd.tensor_tensor(ez[:, :, :], two[:, :, :], z[:, :, :], ALU.pow).then_inc(ez_ready, 1)

            def attn_body(i, n):
                pool.wait_ge(xn_ready, n + 1)
                xt = x[:, bass.ds(i * SUB, SUB), :]
                nc.gpsimd.tensor_tensor(xt, xt, bout_rows[:, :].unsqueeze(1).to_broadcast([P, SUB, C]),
                                        ALU.add).then_inc(bout_added, 1)
                rstd_pow(n + 1)

            rstd_pow(0)
            pool.wait_ge(w1_loaded, 16)
            nc.gpsimd.tensor_copy(w1h[0][:, :, :], w1[0][:, :, :]).then_inc(w1h_ready, 1)
            pool.wait_ge(w1h_ready, 1)
            nc.gpsimd.tensor_tensor(w1l[0][:, :, :], w1[0][:, :, :], w1h[0][:, :, :].bitcast(F32),
                                    ALU.subtract).then_inc(clean_ready, 1)
            pool.wait_ge(cols_loaded, 16 * N_COLS)
            nc.gpsimd.tensor_copy(proj_parts[:, :], proj_copies[:, :]).then_inc(proj_rounded, 1)
            pool.wait_ge(proj_rounded, 1)
            low = slice(P // 2, P)
            nc.gpsimd.tensor_tensor(proj_parts[low, :], proj_copies[low, :], proj_parts[low, :].bitcast(F32),
                                    ALU.subtract).then_inc(feat_w_ready, 1)
            pool.wait_ge(feat_w_ready, 1)
            pool.wait_ge(setup_copied, 4)
            nc.gpsimd.tensor_tensor(wqk_l[:, :, :], wqk_t[:, :, :], wqk_h[:, :, :].bitcast(F32),
                                    ALU.subtract).then_inc(feat_w_ready, 1)
            with pool.Fori(0, NT) as i:
                ffn_body(i, i)
            with pool.Fori(0, NT) as i:
                attn_body(i, i + NT)
            with pool.Fori(0, NT) as i:
                ffn_body(i + NT, i + 2 * NT)

        @block.vector
        def _(dve):
            V = nc.vector
            setup = Steps(dve, setup_step, 0)
            flat = "p c f -> p (c f)"

            def magnitude(dst, src):
                return V.tensor_scalar(dst.bitcast(I32), src.bitcast(I32), 0x7FFFFFFF, None, ALU.bitwise_and)

            def changed(n):
                return max(1, int(n * SPARSITY / 2))

            for g in range(2):
                setup(V.memset(found[g][:, :], 0))
            for g, loaded in enumerate((w1_loaded, w2_loaded)):
                dve.wait_ge(loaded, 16)
                setup(magnitude(mag[g][:, :], (w1, w2)[g][0][:, :, :].rearrange(flat)))

            def compare(g):
                for col in range(2):
                    last = V.tensor_scalar(below[g][:, col, :], mag[g][:, :], trial[g][:, col:col + 1].bitcast(F32),
                                           None, ALU.is_lt)
                last.then_inc(mask_ready, 1)

            def accept(g, b, before):
                dve.wait_ge(tot_ready, before + 1)
                for col, most in enumerate((changed(C * FF) - 1, C * FF - changed(C * FF))):
                    last = V.tensor_scalar(keep[g][:, col:col + 1], TOT_BANK[g][:, col:col + 1], float(most),
                                           bits_f[:, bass.ds(b, 1)], ALU.is_le, ALU.mult)
                return last

            def stats(n, tile):
                for g in range(SUB):
                    V.bn_stats(bn6[:, g, :], x[:, bass.ds(tile * SUB + g, 1), :]).then_inc(stats_step, 1)
                dve.wait_ge(stats_step, SUB * (n + 1))
                V.memset(spare[:, :], 0.0)
                for g in range(SUB):
                    last = V.bn_aggr(mv[:, g, :], bn6[:, g, :])
                last.then_inc(stats_ready, 1)

            dve.wait_ge(x0_loaded, 16)
            stats(0, 0)
            dve.wait_ge(bits_ready, 1)
            step = Steps(dve, search_step, 0)
            for g in range(2):
                step(V.tensor_tensor(trial[g][:, :], found[g][:, :], bits[:, 0:1].to_broadcast([P, 2]), ALU.bitwise_or))
                compare(g)
            with dve.Fori(1, BITS) as b:
                step = Steps(dve, search_step, 6 * (b - 1) + 2)
                for g in range(2):
                    step(accept(g, b - 1, 2 * (b - 1) + g))
                    step(V.scalar_tensor_tensor(out=trial[g][:, :], in0=keep[g][:, :], scalar=bits[:, bass.ds(b, 1)],
                                                in1=found[g][:, :], op0=ALU.bitwise_or, op1=ALU.bitwise_or))
                    compare(g)
                    step.n += 1
                    V.tensor_tensor(found[g][:, :], found[g][:, :], keep[g][:, :], ALU.bitwise_or).then_inc(search_step, 1)
            step = Steps(dve, search_step, 6 * (BITS - 1) + 2)
            for g in range(2):
                step(accept(g, BITS - 1, 2 * (BITS - 1) + g))
                step(V.tensor_tensor(found[g][:, :], found[g][:, :], keep[g][:, :], ALU.bitwise_or))

            def normalise(n, tile):
                dve.wait_ge(rstd_ready, n + 1)
                for g in range(SUB):
                    last = V.tensor_scalar(xn[:, g, :], x[:, bass.ds(tile * SUB + g, 1), :], mv[:, g, 0:1],
                                           rstd[:, g:g + 1], ALU.subtract, ALU.mult)
                last.then_inc(xn_ready, 1)

            def split_xnT(n):
                dve.wait_ge(xnT_ready, n + 1)
                V.tensor_copy(xnTh[:, :], xnT[:, :]).then_inc(xnTh_step, 1)
                dve.wait_ge(xnTh_step, n + 1)
                V.tensor_tensor(xnTl[:, :], xnT[:, :], xnTh[:, :].bitcast(F32), ALU.subtract).then_inc(xnT_split, 1)

            def add_expert(t, e, tile):
                dve.wait_ge(ytok_psum, 2 * t + e + 1)
                for g in range(SUB):
                    xt = x[:, bass.ds(tile * SUB + g, 1), :]
                    last = V.scalar_tensor_tensor(out=xt, in0=YTOK_BANK[:, g * P:(g + 1) * P],
                                                  scalar=prob[:, e, g:g + 1], in1=xt, op0=ALU.mult, op1=ALU.add)
                last.then_inc(y_added, 1)

            def ffn_body(t, n, tile, following, before):
                if before is not None:
                    add_expert(t - 1, 1, before)
                dve.wait_ge(rstd2_ready, t + 1)
                stats(n + 1, following)
                dve.wait_ge(z_psum, t + 1)
                step = Steps(dve, z_step, 3 * t)
                raw = L_BANK[:, P:2 * P].rearrange("p (g w) -> p g w", g=SUB)[:, :, 0:E]
                step(V.tensor_tensor(z[:, :, :], raw, rstd2[:, :].unsqueeze(2).to_broadcast([P, SUB, E]), ALU.mult))
                step(V.tensor_tensor(z[:, :, :], z[:, :, :], logit_b[:, :].unsqueeze(1).to_broadcast([P, SUB, E]), ALU.add))
                step(V.tensor_reduce(zmax[:, :], z[:, :, :], AX_X, ALU.max))
                V.tensor_tensor(z[:, :, :], z[:, :, :], zmax[:, :].unsqueeze(2).to_broadcast([P, SUB, E]),
                                ALU.subtract).then_inc(z_ready, 1)
                dve.wait_ge(xnT_psum, n + 1)
                normalise(n + 1, following)
                dve.wait_ge(ez_ready, t + 1)
                step = Steps(dve, prob_step, 4 * t)
                step(V.tensor_reduce(esum[:, :], ez[:, :, 1:E], AX_X, ALU.add))
                step(V.tensor_tensor(etot[:, :], esum[:, :], ez[:, :, 0], ALU.add))
                step(V.reciprocal(erec[:, :], etot[:, :]))
                V.scalar_tensor_tensor(out=prob[:, 0, :], in0=ez[:, :, 0], scalar=0.5, in1=erec[:, :],
                                       op0=ALU.mult, op1=ALU.mult)
                step(V.scalar_tensor_tensor(out=prob[:, 1, :], in0=esum[:, :], scalar=0.5, in1=erec[:, :],
                                            op0=ALU.mult, op1=ALU.mult))
                dve.wait_ge(hid_psum, K2 * (t + 1))
                split_xnT(n + 1)
                add_expert(t, 0, tile)

            def scores_masked(i, m):
                dve.wait_ge(score_psum, COMBOS * i + m + 1)
                if m >= 4:
                    dve.wait_ge(aw_used, COMBOS * i + m - 3)
                V.tensor_tensor(aw[m % 4][:, :], S_BANK[m % 3][:, 0:AW], causal[:, :], ALU.mult).then_inc(aw_ready, 1)

            def ctx_normalised(i, g):
                dve.wait_ge(ctok_psum, GROUPS * i + g + 1)
                raw = T_BANK[:, :].rearrange("p (s j w) -> p s j w", s=SUB, j=HG)
                step = Steps(dve, norm_ctx_step, 2 * (GROUPS * i + g))
                step(V.tensor_scalar(den[:, :, :], raw[:, :, :, D], DELTA, None, ALU.add))
                step(V.reciprocal(rden[:, :, :], den[:, :, :]))
                part = ctxn[:, :, g * HG * D:(g + 1) * HG * D].rearrange("p s (j d) -> p s j d", j=HG)
                V.tensor_tensor(part, raw[:, :, :, 0:D], rden[:, :, :].unsqueeze(3).to_broadcast([P, SUB, HG, D]),
                                ALU.mult).then_inc(ctxn_ready, 1)

            def attn_finished(i, tile):
                dve.wait_ge(attn_psum, i + 1)
                dve.wait_ge(bout_added, i + 1)
                xt = x[:, bass.ds(tile * SUB, SUB), :]
                V.tensor_tensor(xt, X_BANK[:, :].rearrange("p (s c) -> p s c", s=SUB), xt, ALU.add).then_inc(attn_added, 1)

            def qk_low(i, a):
                dve.wait_ge(qk_high_ready, 2 * i + a + 1)
                V.scalar_tensor_tensor(out=qk_part[1][:, a, :], in0=X_BANK[:, :], scalar=bqk_sb[:, a:a + 1],
                                       in1=qk_part[0][:, a, :].bitcast(F32), op0=ALU.add,
                                       op1=ALU.subtract).then_inc(qk_low_ready, 1)

            def attn_body(i, n, following, before):
                dve.wait_ge(v_psum, i + 1)
                V.tensor_tensor(v_aug[:, :, :, 0:D], X_BANK[:, :].rearrange("p (s h d) -> p s h d", s=SUB, h=H),
                                bv_rows[:, :].rearrange("p (h d) -> p h d", h=H).unsqueeze(1).to_broadcast([P, SUB, H, D]),
                                ALU.add).then_inc(v_ready, 1)
                for m in range(COMBOS):
                    scores_masked(i, m)
                    if m == 1 and before is not None:
                        ctx_normalised(i - 1, GROUPS - 1)
                    if m == 9 and before is not None:
                        attn_finished(i - 1, before)
                    if m >= 13 and m % 8 == 5:
                        ctx_normalised(i, (m - 13) // 8)
                    if m == 4:
                        stats(n + 1, following)
                    if m == 11:
                        dve.wait_ge(xnT_psum, n + 1)
                        normalise(n + 1, following)
                    if m == 16:
                        split_xnT(n + 1)
                    if m in (20, 24):
                        qk_low(i + 1, m // 4 - 5)

            normalise(0, 0)
            dve.wait_ge(const_ready, 1)
            dve.wait_ge(w_loaded, 16 * N_W)
            dve.wait_ge(cols_loaded, 16 * N_COLS)
            setup(V.tensor_scalar(wr_g[:, 0:E], wr_sb[:, :], gamma_sb[:, 0:1], LOG2E, ALU.mult, ALU.mult))
            setup(V.tensor_scalar(wr_l[:, :], wr_sb[:, :], LOG2E, None, ALU.mult))
            setup(V.tensor_copy(beta_wide[:, :], beta_sb[:, 0:1].to_broadcast([P, P])))
            split_xnT(0)
            dve.wait_ge(logit_b_psum, 1)
            V.scalar_tensor_tensor(out=logit_b[:, :], in0=br_rows[:, :], scalar=LOG2E, in1=bk[1][:, 64:64 + E],
                                   op0=ALU.mult, op1=ALU.add).then_inc(logit_b_copied, 1)

            step = Steps(dve, perturb_step, 0)
            def perturb(top, bot, clean, pert):
                step(V.scalar_tensor_tensor(out=bot, in0=top, scalar=-2.0, in1=bot, op0=ALU.mult, op1=ALU.add))
                step(V.tensor_scalar(top, clean, SCALE, None, ALU.mult))
                step(V.scalar_tensor_tensor(out=bot, in0=bot, scalar=-1.0, in1=top, op0=ALU.max, op1=ALU.mult))
                step(V.tensor_tensor(pert, clean, bot, ALU.add))

            def perturb_matrix(g, w):
                step(V.tensor_scalar(mask_top[:, :], mag[g][:, :], found[g][:, 1:2].bitcast(F32), None, ALU.is_ge))
                step(V.tensor_scalar(mask_bot[:, :], mag[g][:, :], found[g][:, 0:1].bitcast(F32), None, ALU.is_le))
                perturb(mask_top[:, :], mask_bot[:, :], w[0][:, :, :].rearrange(flat), w[1][:, :, :].rearrange(flat))

            perturb_matrix(0, w1)
            V.tensor_copy(w1h[1][:, :, :], w1[1][:, :, :]).then_inc(w1h_p_ready, 1)
            dve.wait_ge(w1h_p_ready, 1)
            V.tensor_tensor(w1l[1][:, :, :], w1[1][:, :, :], w1h[1][:, :, :].bitcast(F32), ALU.subtract).then_inc(weights_ready, 1)
            perturb_matrix(1, w2)
            V.memset(spare[:, :], 0.0).then_inc(weights_ready, 1)

            dve.wait_ge(b_loaded, 16 * N_B)
            for dst, src in ((ab1, b1c[0]), (ab2, b2c[0]), (ab1_row, ab1_row), (ab2_row, ab2_row)):
                step(magnitude(dst[:, :], src[:, :]))
            for c in range(FC + 1):
                one, every = (ab1[:, c:c + 1], ab1_row) if c < FC else (ab2[:, 0:1], ab2_row)
                for n_, op in ((n_less, ALU.is_lt), (n_more, ALU.is_gt)):
                    step(V.tensor_scalar(junk[:, 0:every.shape[1]], every[:, :], one, None, op, ALU.add,
                                         accum_out=n_[:, c:c + 1]))

            for cols, clean, pert, n_b in ((slice(0, FC), b1c[0], b1c[1], FF), (slice(FC, FC + 1), b2c[0], b2c[1], C)):
                w = clean.shape[1]
                few = changed(n_b) - 1
                step(V.tensor_scalar(mask_top[:, 0:w], n_more[:, cols], float(few), None, ALU.is_le))
                step(V.tensor_scalar(mask_bot[:, 0:w], n_less[:, cols], float(few), None, ALU.is_le))
                perturb(mask_top[:, 0:w], mask_bot[:, 0:w], clean[:, :], pert[:, :])
            V.memset(spare[:, :], 0.0).then_inc(b_ready, 1)
            dve.wait_ge(x_loaded, 16 * N_X)
            ffn_body(0, 0, 0, 1, None)
            with dve.Fori(1, NT) as i:
                ffn_body(i, i, i, (i + 1) % NT, i - 1)
            add_expert(NT - 1, 1, NT - 1)
            qk_low(0, 0)
            qk_low(0, 1)
            attn_body(0, NT, 1, None)
            with dve.Fori(1, NT) as i:
                attn_body(i, i + NT, (i + 1) % NT, i - 1)
            ctx_normalised(NT - 1, GROUPS - 1)
            attn_finished(NT - 1, NT - 1)
            ffn_body(NT, 2 * NT, 0, 1, None)
            with dve.Fori(1, NT) as i:
                ffn_body(i + NT, i + 2 * NT, i, (i + 1) % NT, i - 1)
            add_expert(2 * NT - 1, 1, NT - 1)

        @block.tensor
        def _(pe):
            mm = nc.tensor.matmul
            pe.wait_ge(const_ready, 1)
            with pe.Fori(0, BITS) as b:
                for g in range(2):
                    pe.wait_ge(mask_ready, 2 * b + g + 1)
                    for col in range(2):
                        for c in range(FC):
                            last = mm(CNT_BANK[g][:, col:col + 1], below[g][:, col, c * P:(c + 1) * P],
                                      ones16[:, 0:1], start=(c == 0), stop=(c == FC - 1))
                    last.then_inc(cnt_psum, 1)
                    pe.wait_ge(cnt_ready, 2 * b + g + 1)
                    mm(TOT_BANK[g][:, 0:2], ones16[:, :], cnt[g][:, :], start=True, stop=True).then_inc(tot_ready, 1)
            def xn_transposed(n):
                pe.wait_ge(xn_ready, n + 1)
                for g in range(SUB):
                    last = nc.tensor.transpose(X_BANK[:, g * P:(g + 1) * P], xn[:, g, :], ident[:, :])
                last.then_inc(xnT_psum, 1)

            def mm3(dst, wh, wl):
                mm(dst, wh, xnTh[:, :], start=True, stop=False)
                mm(dst, wh, xnTl[:, :], start=False, stop=False)
                return mm(dst, wl, xnTh[:, :], start=False, stop=True)

            def y_transposed(t, e):
                pe.wait_ge(y_ready, 2 * t + e + 1)
                pe.wait_ge(y_added, 2 * t + e + 1)
                for g in range(SUB):
                    last = nc.tensor.transpose(YTOK_BANK[:, g * P:(g + 1) * P], yT[e][:, g * P:(g + 1) * P],
                                               ident[:, :])
                last.then_inc(ytok_psum, 1)

            def ffn_body(t, n, first):
                def hidden(k):
                    e, c = divmod(k, FC)
                    if k >= 3:
                        pe.wait_ge(hid_ready, K2 * t + k - 2)
                    mm3(H_BANK[k % 3][:, :], w1h[e][:, c, :], w1l[e][:, c, :]).then_inc(hid_psum, 1)

                def output(k):
                    e, c = divmod(k, FC)
                    pe.wait_ge(hid_ready, K2 * t + k + 1)
                    last = mm(Y_BANK[e][:, :], w2[e][:, c, :], hid[k % 4][:, :], start=(c == 0), stop=(c == FC - 1))
                    last.then_inc(hid_used, 1)

                pe.wait_ge(xnT_split, n + 1)
                hidden(0)
                hidden(1)
                for g in range(SUB):
                    last = mm(L_BANK[g * VW:(g + 1) * VW, 0:P], wr_g[:, :], xnT[:, g * P:(g + 1) * P],
                              start=True, stop=True, tile_position=(0, g * VW))
                last.then_inc(logT_psum, 1)
                if not first:
                    y_transposed(t - 1, 1)
                hidden(2)
                output(0)
                pe.wait_ge(logT_ready, t + 1)
                nc.tensor.transpose(L_BANK[:, P:2 * P], logT[:, :], ident[:, :]).then_inc(z_psum, 1)
                for k in range(3, K2):
                    if k == FC and isinstance(t, int) and t == 0:
                        pe.wait_ge(weights_ready, 1)
                    hidden(k)
                    if k == 6 and isinstance(t, int) and t == 0:
                        pe.wait_ge(weights_ready, 2)
                    if k == 5:
                        xn_transposed(n + 1)
                    output(k - 2)
                    if k == 6:
                        y_transposed(t, 0)
                output(6)
                output(7)

            def ctx_transposed(i, g):
                pe.wait_ge(ctxT_ready, GROUPS * i + g + 1)
                if g >= 1:
                    pe.wait_ge(ctxn_ready, GROUPS * i + g)
                for s in range(SUB):
                    last = nc.tensor.transpose(T_BANK[:, s * P:(s + 1) * P], ctxT[g % 2][:, s * P:(s + 1) * P],
                                               ident[:, :])
                last.then_inc(ctok_psum, 1)

            def ctxn_transposed(i):
                pe.wait_ge(ctxn_ready, GROUPS * (i + 1))
                for s in range(SUB):
                    last = nc.tensor.transpose(T_BANK[:, s * P:(s + 1) * P], ctxn[:, s, :], ident[:, :])
                last.then_inc(ctxnT_psum, 1)

            def projected(i):
                pe.wait_ge(ctxnT_ready, i + 1)
                for s in range(SUB):
                    last = mm(X_BANK[:, s * P:(s + 1) * P], ctxnT[:, s * P:(s + 1) * P], wout_t[:, :],
                              start=True, stop=True)
                last.then_inc(attn_psum, 1)

            def qk_projected(i, a):
                if a == 1:
                    pe.wait_ge(qk_low_ready, 2 * i + 1)
                mm3(X_BANK[:, :], wqk_h[:, a, :], wqk_l[:, a, :]).then_inc(qk_psum, 1)

            def attn_body(i, n, first):
                def features(p):
                    if p % 2 == 0:
                        pe.wait_ge(stacked[p // 2], 16 * COPIES * (i + 1))
                    if p >= 1:
                        pe.wait_ge(feat_ready, 2 * (PAIRS * i + p))
                    for a, dst in enumerate((Q_BANK, KEY_BANK)):
                        mm(dst[:, :], proj_parts[:, p * P:(p + 1) * P], qk_stack[:, a, p // 2, :], start=True,
                           stop=True).then_inc(feat_psum, 1)

                def scores(m):
                    p, b, e = m // 4, m // 2 % 2, m % 2
                    rows = slice(e * M, (e + 1) * M)
                    if m % 4 == 0:
                        pe.wait_ge(feat_ready, 2 * (PAIRS * i + p + 1))
                    if m >= 3:
                        pe.wait_ge(aw_ready, COMBOS * i + m - 2)
                    q, k, o = qf[p % 2], kf[p % 2], S_BANK[m % 3]
                    mm(o[:, 0:S], k[rows, b * S:b * S + P], q[rows, b * S:(b + 1) * S], start=True, stop=True)
                    mm(o[:, S:AW], k[rows, b * S + P:(b + 1) * S], q[rows, b * S + P:(b + 1) * S],
                       start=True, stop=True).then_inc(score_psum, 1)

                def context(m):
                    p, b, e = m // 4, m // 2 % 2, m % 2
                    g, j = divmod(2 * p + e, HG)
                    if m == 0:
                        pe.wait_ge(v_ready, i + 1)
                    if m % 8 == 0 and m > 0:
                        pe.wait_ge(ctxT_ready, GROUPS * i + g)
                    pe.wait_ge(aw_ready, COMBOS * i + m + 1)
                    rows = slice(j * VW, (j + 1) * VW)
                    h = 2 * p + e
                    mm(C_BANK[rows, b * S:(b + 1) * S], v_aug[:, 2 * b, h, :], aw[m % 4][:, 0:S], start=True,
                       stop=False, tile_position=(0, j * VW))
                    last = mm(C_BANK[rows, b * S + P:(b + 1) * S], v_aug[:, 2 * b + 1, h, :], aw[m % 4][:, S:AW],
                              start=False, stop=True, tile_position=(0, j * VW))
                    last.then_inc(aw_used, 1)

                features(0)
                pe.wait_ge(qk_low_ready, 2 * (i + 1))
                for s in range(SUB):
                    last = mm(X_BANK[:, s * P:(s + 1) * P], xnT[:, s * P:(s + 1) * P], wv_t[:, :], start=True, stop=True)
                last.then_inc(v_psum, 1)
                for m in range(COMBOS):
                    if m % 4 == 0 and m // 4 + 1 < PAIRS:
                        features(m // 4 + 1)
                    scores(m)
                    if m >= 2:
                        context(m - 2)
                    if not first:
                        if m == 1:
                            ctx_transposed(i - 1, GROUPS - 1)
                        if m == 4:
                            ctxn_transposed(i - 1)
                        if m == 8:
                            pe.wait_ge(v_ready, i + 1)
                            projected(i - 1)
                    if m >= 12 and m % 8 == 4:
                        ctx_transposed(i, (m - 12) // 8)
                    if m == 12:
                        if first:
                            pe.wait_ge(v_ready, 1)
                        else:
                            pe.wait_ge(attn_added, i)
                        xn_transposed(n + 1)
                    if m == 18:
                        pe.wait_ge(xnT_split, n + 2)
                        qk_projected(i + 1, 0)
                    if m == 22:
                        qk_projected(i + 1, 1)
                context(COMBOS - 2)
                context(COMBOS - 1)

            xn_transposed(0)
            pe.wait_ge(w_loaded, 16 * N_W)
            pe.wait_ge(cols_loaded, 16 * N_COLS)
            nc.tensor.transpose(bk[0][:, 0:P], wqkv_sb[:, 2, :], ident[:, :])
            nc.tensor.transpose(bk[0][:, P:2 * P], wout_sb[:, :], ident[:, :])
            for a in range(2):
                last = nc.tensor.transpose(bk[0][:, (2 + a) * P:(3 + a) * P], wqkv_sb[:, a, :], ident[:, :])
            last.then_inc(setup_psum, 1)
            pe.wait_ge(setup_step, 7)
            mm(bk[1][:, 64:64 + E], beta_wide[:, :], wr_l[:, :], start=True, stop=True).then_inc(logit_b_psum, 1)
            pe.wait_ge(clean_ready, 1)
            pe.wait_ge(setup_copied, 4)
            pe.wait_ge(logit_b_copied, 1)
            ffn_body(0, 0, True)
            with pe.Fori(1, NT) as i:
                ffn_body(i, i, False)
            y_transposed(NT - 1, 1)
            pe.wait_ge(y_added, 2 * NT + 1)
            pe.wait_ge(feat_w_ready, 2)
            pe.wait_ge(xnT_split, NT + 1)
            qk_projected(0, 0)
            qk_projected(0, 1)
            attn_body(0, NT, True)
            with pe.Fori(1, NT) as i:
                attn_body(i, i + NT, False)
            ctx_transposed(NT - 1, GROUPS - 1)
            ctxn_transposed(NT - 1)
            projected(NT - 1)
            pe.wait_ge(attn_added, NT)
            ffn_body(NT, 2 * NT, True)
            with pe.Fori(1, NT) as i:
                ffn_body(i + NT, i + 2 * NT, False)
            y_transposed(2 * NT - 1, 1)


_INS = ["L0_attn_x", "L0_attn_Wqkv", "L0_attn_bqkv", "L0_attn_Wout", "L0_attn_bout", "L0_attn_proj", "L0_ffn_W1",
        "L0_ffn_b1", "L0_ffn_W2", "L0_ffn_b2", "L0_ffn_ln_gamma", "L0_ffn_ln_beta", "L0_ffn_Wr", "L0_ffn_br"]


def kernel(**inputs):
    import numpy as np
    import concourse.bacc as bacc
    from concourse.bass_utils import run_bass_kernel_spmd

    nc = bacc.Bacc("TRN2", target_bir_lowering=False, num_devices=1)
    arrays, args = {}, []
    for name in _INS:
        a = np.ascontiguousarray(inputs[name])
        arrays["in_" + name] = a
        args.append(nc.dram_tensor("in_" + name, a.shape, mybir.dt.from_np(a.dtype), kind="ExternalInput").ap())
    shape = arrays["in_L0_attn_x"].shape
    out = nc.dram_tensor("out_x", shape, F32, kind="ExternalOutput").ap()
    macaron_kernel(nc, *args, out)
    r = run_bass_kernel_spmd(nc, [arrays], core_ids=[0])
    return r.results[0]["out_x"]
```

```python
import math
from contextlib import ExitStack

import concourse.bass as bass
from concourse import mybir

F32 = mybir.dt.float32
F16 = mybir.dt.float16
F32R = mybir.dt.float32r
I32 = mybir.dt.int32
ALU = mybir.AluOpType
ACT = mybir.ActivationFunctionType
AX_X = mybir.AxisListType.X

P = 128
EPS = 1e-5
DELTA = 1e-6
LOG2E = math.log2(math.e)
SCALE, SPARSITY = 0.8, 0.1


class Steps:

    def __init__(self, eng, sem, before):
        self.eng, self.sem, self.before, self.n = eng, sem, before, 0

    def __call__(self, ins):
        self.n += 1
        ins.then_inc(self.sem, 1)
        self.eng.wait_ge(self.sem, self.before + self.n)


def changed(n):
    return max(1, int(n * SPARSITY / 2))


def macaron_kernel(nc, x_in, Wqkv, bqkv, Wout, bout, proj, W1, b1, W2, b2, gamma, beta, Wr, br, out):
    B, S, C = x_in.shape
    H, D, M = proj.shape
    FF = W1.shape[1]
    E = Wr.shape[1]
    G = B * S // P
    SUB = 4
    T = SUB * P
    NT = G // SUB
    NSEQ = T // S
    FC = FF // P
    K2 = 2 * FC
    PAIRS = H // 2
    COMBOS = NSEQ * H
    HG = 4
    GROUPS = H // HG
    STEPS = COMBOS // 2
    BATCHES = GROUPS * NSEQ
    AW_BUFS = 4 * HG
    COPIES = P // (HG * D)
    VW = 32
    AW = S + P
    RANKS = (changed(C * FF) - 1, C * FF - changed(C * FF))
    assert C == P and H * D == P and S == 2 * P and 2 * M == P and NSEQ == 2 and FC == 4

    x_dram = x_in.rearrange("b (g p) c -> p (b g) c", p=P)
    out_dram = out.rearrange("b (g p) c -> p (b g) c", p=P)

    with ExitStack() as ctx:
        def sb(name, shape, dt=F32):
            return ctx.enter_context(nc.sbuf_tensor(name, shape, dt))

        def bank(name):
            return ctx.enter_context(nc.psum_tensor(name, [P, 512], F32))

        def sem(name):
            return ctx.enter_context(nc.semaphore(name))

        x = sb("x_all", [P, G, C])
        ident = sb("ident", [P, P])
        causal = sb("causal", [P, AW])
        w1 = [sb("w1_clean", [P, FC, P]), sb("w1_perturbed", [P, FC, P])]
        w2 = [sb("w2_clean", [P, FC, P]), sb("w2_perturbed", [P, FC, P])]
        b1c = [sb("b1_clean", [P, FC]), sb("b1_perturbed", [P, FC])]
        b2c = [sb("b2_clean", [P, 1]), sb("b2_perturbed", [P, 1])]
        wqkv_sb = sb("wqkv_sb", [P, 3, C])
        wout_sb = sb("wout_sb", [P, C])
        bqk_sb = sb("bqk_sb", [P, 2])
        proj_copies = sb("proj_copies", [P, H * M])
        wr_sb = sb("wr_sb", [P, E])
        gamma_sb = sb("gamma_sb", [P, 1])
        beta_sb = sb("beta_sb", [P, 1])
        bv_rows = sb("bv_rows", [P, C])
        bout_rows = sb("bout_rows", [P, C])
        br_rows = sb("br_rows", [P, E])
        wv_t = sb("wv_t", [P, C])
        wout_t = sb("wout_t", [P, C])
        wqk_t = sb("wqk_t", [P, 2, C])
        wqk_h = sb("wqk_h", [P, 2, C], F32R)
        wqk_l = sb("wqk_l", [P, 2, C], F32R)
        proj_parts = sb("proj_parts", [P, H * M], F32R)
        w1h = [sb("w1h_clean", [P, FC, P], F32R), sb("w1h_perturbed", [P, FC, P], F32R)]
        w1l = [sb("w1l_clean", [P, FC, P], F32R), sb("w1l_perturbed", [P, FC, P], F32R)]
        wr_g = sb("wr_g", [P, VW])
        beta_wide = sb("beta_wide", [P, P])
        wr_l = sb("wr_l", [P, E])
        logit_b = sb("logit_b", [P, E])
        BITS = 31
        mag = [sb("abs_w1", [P, FF]), sb("abs_w2", [P, FF])]
        ab1 = sb("abs_b1", [P, FC])
        ab2 = sb("abs_b2", [P, 1])
        ab1_row = sb("abs_b1_row", [P, FF])
        ab2_row = sb("abs_b2_row", [P, C])
        below = [sb(f"below{g}", [P, 2, FF], F16) for g in range(2)]
        scaled = [sb("scaled_w1", [P, FF]), sb("scaled_w2", [P, FF])]
        tier = sb("tier", [P, FF])
        b_scaled = sb("b_scaled", [P, FC])
        b_tier = sb("b_tier", [P, FC])
        compared = sb("compared", [P, 2, FC + 1, FF], F16)
        ones16 = sb("ones16", [P, P], F16)
        found = [sb(f"found{g}", [P, 2], I32) for g in range(2)]
        trial = [sb(f"trial{g}", [P, 2], I32) for g in range(2)]
        keep = [sb(f"keep{g}", [P, 2], I32) for g in range(2)]
        minus_most = sb("minus_most", [P, 2, 2], F16)
        cnt = [sb(f"cnt{g}", [P, 2], F16) for g in range(2)]
        bits = sb("bits", [P, BITS], I32)
        bits_f = sb("bits_f", [P, BITS])
        n_less = sb("n_less", [P, FC + 1])
        n_more = sb("n_more", [P, FC + 1])
        bn6 = sb("bn6", [P, SUB, 6])
        mv = sb("mean_var", [P, SUB, 2])
        minus_half = sb("minus_half", [P, SUB])
        var_eps = sb("var_eps", [P, SUB])
        eps_tile = sb("eps_tile", [P, SUB])
        spare = sb("spare", [P, 1])
        gelu_warm = sb("gelu_warm", [P, 1])
        rstd = sb("rstd", [P, SUB])
        ratio = sb("ratio", [P, SUB])
        rstd2 = sb("rstd2", [P, SUB])
        xn = sb("xn", [P, SUB, C])
        xnT = sb("xnT", [P, T])
        xnTh = sb("xnTh", [P, T], F32R)
        xnTl = sb("xnTl", [P, T], F32R)
        v_aug = sb("v_aug", [P, SUB, H, VW])
        z_all = sb("z_all", [P, G, E])
        zmax_all = sb("zmax_all", [P, G])
        ez_all = sb("ez_all", [P, G, E])
        rstd2_all = sb("rstd2_all", [P, G])
        two = sb("two", [P, SUB, E])
        logT = sb("logT", [P, P])
        z = sb("z", [P, SUB, E])
        zmax = sb("zmax", [P, SUB])
        ez = sb("ez", [P, SUB, E])
        esum = sb("esum", [P, SUB])
        etot = sb("etot", [P, SUB])
        erec = sb("erec", [P, SUB])
        prob = sb("prob", [P, 2, SUB])
        hid = [sb(f"hid{i}", [P, T]) for i in range(4)]
        yT = [sb(f"yT{i}", [P, T]) for i in range(2)]
        with ExitStack() as first_ffn:
            xnT_all = first_ffn.enter_context(nc.sbuf_tensor("xnT_all", [P, NT, T], F32))
            ytok_all = first_ffn.enter_context(nc.sbuf_tensor("ytok_all", [P, NT, SUB, C], F32))
        qk_part = [sb("qk_high", [P, 2, T], F32R), sb("qk_low", [P, 2, T], F32R)]
        qk_stack = sb("qk_stack", [P, 2, GROUPS, T], F32R)
        qf = [sb(f"qf{i}", [P, T]) for i in range(2)]
        kf = [sb(f"kf{i}", [P, T]) for i in range(2)]
        aw = [sb(f"aw{i}", [P, AW]) for i in range(AW_BUFS)]
        ctxT = [sb(f"ctxT{i}", [P, T]) for i in range(2)]
        den = sb("den", [P, SUB, HG])
        rden = sb("rden", [P, SUB, HG])
        ctxn = sb("ctxn", [P, SUB, C])
        ctxnT = sb("ctxnT", [P, T])

        bk = [bank(f"bank{i}") for i in range(8)]
        X_BANK = bk[7]
        CNT_BANK = [bk[4], bk[5]]
        TOT = 4
        TOK_BANK = bk[2]
        H_BANK = [bk[0], bk[1], bk[2]]
        Y_BANK = [bk[3], bk[4]]
        YTOK_BANK = bk[5]
        L_BANK = bk[6]
        Q_BANK, KEY_BANK = bk[0], bk[1]
        S_BANK = [bk[2], bk[3], bk[4]]
        C_BANK = bk[5]
        T_BANK = bk[6]

        w1_loaded = sem("w1_loaded")
        w2_loaded = sem("w2_loaded")
        w_loaded = sem("w_loaded")
        cols_loaded = sem("cols_loaded")
        proj_loaded = sem("proj_loaded")
        x0_loaded = sem("x0_loaded")
        x1_loaded = sem("x1_loaded")
        x_loaded = sem("x_loaded")
        proj_zeroed = sem("proj_zeroed")
        const_step = sem("const_step")
        const_ready = sem("const_ready")
        setup_step = sem("setup_step")
        setup_psum = sem("setup_psum")
        setup_copied = sem("setup_copied")
        search_step = sem("search_step")
        mask_ready = sem("mask_ready")
        cnt_psum = sem("cnt_psum")
        cnt_ready = sem("cnt_ready")
        tot_ready = sem("tot_ready")
        b_loaded = sem("b_loaded")
        bits_ready = sem("bits_ready")
        logit_b_psum = sem("logit_b_psum")
        logit_b_copied = sem("logit_b_copied")
        perturb_step = sem("perturb_step")
        weights_ready = sem("weights_ready")
        stats_step = sem("stats_step")
        stats_ready = sem("stats_ready")
        norm_step = sem("norm_step")
        rstd_ready = sem("rstd_ready")
        xn_ready = sem("xn_ready")
        xnT_psum = sem("xnT_psum")
        xnT_ready = sem("xnT_ready")
        xnTh_step = sem("xnTh_step")
        xnT_split = sem("xnT_split")
        w1h_ready = sem("w1h_ready")
        w1h_p_ready = sem("w1h_p_ready")
        clean_ready = sem("clean_ready")
        proj_rounded = sem("proj_rounded")
        feat_w_ready = sem("feat_w_ready")
        b_ready = sem("b_ready")
        ratio_step = sem("ratio_step")
        rstd2_ready = sem("rstd2_ready")
        logT_psum = sem("logT_psum")
        logT_ready = sem("logT_ready")
        z_psum = sem("z_psum")
        z_step = sem("z_step")
        z_ready = sem("z_ready")
        z_raw_ready = sem("z_raw_ready")
        z_all_step = sem("z_all_step")
        z_all_ready = sem("z_all_ready")
        xnT_kept = sem("xnT_kept")
        ytok_kept = sem("ytok_kept")
        again_step = sem("again_step")
        xnT_split_again = sem("xnT_split_again")
        bias_step = sem("bias_step")
        scaled_ready = sem("scaled_ready")
        b_perturb_step = sem("b_perturb_step")
        ez_ready = sem("ez_ready")
        prob_step = sem("prob_step")
        hid_psum = sem("hid_psum")
        hid_ready = sem("hid_ready")
        hid_used = sem("hid_used")
        y_ready = sem("y_ready")
        ytok_psum = sem("ytok_psum")
        y_added = sem("y_added")
        qk_psum = sem("qk_psum")
        qk_high_ready = sem("qk_high_ready")
        qk_low_ready = sem("qk_low_ready")
        stacked = [sem(f"stacked{g}") for g in range(GROUPS)]
        feat_psum = sem("feat_psum")
        feat_ready = sem("feat_ready")
        v_psum = sem("v_psum")
        v_ready = sem("v_ready")
        score_psum = sem("score_psum")
        aw_ready = sem("aw_ready")
        aw_used = sem("aw_used")
        ctxT_ready = sem("ctxT_ready")
        ctok_psum = sem("ctok_psum")
        norm_ctx_step = sem("norm_ctx_step")
        ctxn_ready = sem("ctxn_ready")
        ctxnT_psum = sem("ctxnT_psum")
        ctxnT_ready = sem("ctxnT_ready")
        attn_psum = sem("attn_psum")
        attn_added = sem("attn_added")
        bout_added = sem("bout_added")
        stored = sem("stored")

        N_W, N_COLS, N_PROJ, N_B, N_X = 3, 7, COPIES * HG, FC + 3, 7
        XL = (G - 2 * SUB) // N_X

        block = ctx.enter_context(nc.Block())

        @block.sync
        def _(sp):
            sp.dma_start(w1[0][:, :, :], W1.rearrange("h (c f) -> h c f", c=FC)).then_inc(w1_loaded, 16)
            sp.dma_start(w2[0][:, :, :], W2.rearrange("(c f) h -> f c h", c=FC)).then_inc(w2_loaded, 16)
            sp.dma_start(wqkv_sb[:, :, :], Wqkv.rearrange("(a o) c -> o a c", a=3)).then_inc(w_loaded, 16)
            sp.dma_start(wout_sb[:, :], Wout).then_inc(w_loaded, 16)
            sp.dma_start(wr_sb[:, :], Wr).then_inc(w_loaded, 16)
            sp.dma_start(x[:, 0:SUB, :], x_dram[:, 0:SUB, :]).then_inc(x0_loaded, 16)
            sp.dma_start(x[:, SUB:2 * SUB, :], x_dram[:, SUB:2 * SUB, :]).then_inc(x1_loaded, 16)
            sp.wait_ge(cols_loaded, 16 * N_COLS)
            for lo in range(2 * SUB, G, XL):
                sp.dma_start(x[:, lo:lo + XL, :], x_dram[:, lo:lo + XL, :]).then_inc(x_loaded, 16)
            sp.wait_ge(proj_zeroed, 1)
            for c in range(COPIES):
                for j in range(HG):
                    lo = c * HG * D + j * D
                    sp.dma_start(proj_copies[lo:lo + D, :].rearrange("d (g j m) -> d g j m", j=HG, m=M)[:, :, j, :],
                                 proj.rearrange("(g j) d m -> d g j m", j=HG)[:, :, j, :]).then_inc(proj_loaded, 16)

            def stack(i, first):
                sp.wait_ge(qk_low_ready, 2 * (i + 1))
                for g in range(GROUPS):
                    if not first:
                        sp.wait_ge(feat_psum, 2 * PAIRS * (i - 1) + 4 * (g + 1))
                    for c in range(COPIES):
                        rows, channels = (slice(n * HG * D, (n + 1) * HG * D) for n in (c, g))
                        sp.dma_start(qk_stack[rows, :, g, :].bitcast(F32),
                                     qk_part[c % 2][channels, :, :].bitcast(F32)).then_inc(stacked[g], 16)

            stack(0, True)
            with sp.Fori(1, NT) as i:
                stack(i, False)
            with sp.Fori(0, NT) as i:
                sp.wait_ge(y_added, 2 * (i + NT) + 3)
                sp.dma_start(out_dram[:, bass.ds(i * SUB, SUB), :], x[:, bass.ds(i * SUB, SUB), :]).then_inc(stored, 16)
            sp.wait_ge(stored, 16 * NT)

        @block.scalar
        def _(act):
            column = lambda v: v.rearrange("(f a) -> f a", a=1)
            row = lambda v, n: v.rearrange("(a c) -> a c", a=1).to_broadcast([P, n])
            for c in range(FC):
                act.dma_start(b1c[0][:, c:c + 1], column(b1[c * P:(c + 1) * P])).then_inc(b_loaded, 16)
            act.dma_start(b2c[0][:, :], column(b2)).then_inc(b_loaded, 16)
            act.dma_start(ab1_row[:, :], row(b1, FF)).then_inc(b_loaded, 16)
            act.dma_start(ab2_row[:, :], row(b2, C)).then_inc(b_loaded, 16)
            for a in range(2):
                act.dma_start(bqk_sb[:, a:a + 1], column(bqkv[a * C:(a + 1) * C])).then_inc(cols_loaded, 16)
            act.dma_start(gamma_sb[:, :], column(gamma)).then_inc(cols_loaded, 16)
            act.dma_start(beta_sb[:, :], column(beta)).then_inc(cols_loaded, 16)
            act.dma_start(bv_rows[:, :], row(bqkv[2 * C:3 * C], C)).then_inc(cols_loaded, 16)
            act.dma_start(bout_rows[:, :], row(bout, C)).then_inc(cols_loaded, 16)
            act.dma_start(br_rows[:, :], row(br, E)).then_inc(cols_loaded, 16)

            def xnT_copy(n):
                act.wait_ge(xnT_psum, n + 1)
                nc.scalar.copy(xnT[:, :], X_BANK[:, :]).then_inc(xnT_ready, 1)

            def ffn_body(t, n):
                for k in range(K2):
                    e, c = divmod(k, FC)
                    if k == 6:
                        xnT_copy(n + 1)
                    act.wait_ge(hid_psum, K2 * t + k + 1)
                    if k >= 4:
                        act.wait_ge(hid_used, K2 * t + k - 3)
                    nc.scalar.activation(hid[k % 4][:, :], H_BANK[k % 3][:, :], ACT.Gelu_apprx_tanh,
                                         bias=b1c[e][:, c:c + 1]).then_inc(hid_ready, 1)
                    if k == 1:
                        act.wait_ge(logT_psum, t + 1)
                        nc.scalar.copy(logT[:, :], L_BANK[:, 0:P]).then_inc(logT_ready, 1)
                    if k == 5:
                        act.wait_ge(hid_used, K2 * t + FC)
                        nc.scalar.activation(yT[0][:, :], Y_BANK[0][:, :], ACT.Identity,
                                             bias=b2c[0][:, 0:1]).then_inc(y_ready, 1)
                act.wait_ge(hid_used, K2 * (t + 1))
                nc.scalar.activation(yT[1][:, :], Y_BANK[1][:, :], ACT.Identity,
                                     bias=b2c[1][:, 0:1]).then_inc(y_ready, 1)

            def cnt_copy(b, g):
                act.wait_ge(cnt_psum, 2 * b + g + 1)
                nc.scalar.copy(cnt[g][:, :], CNT_BANK[g][:, 0:2]).then_inc(cnt_ready, 1)

            def ytok_keep(t):
                act.wait_ge(ytok_psum, t + 1)
                nc.scalar.copy(ytok_all[:, bass.ds(t, 1), :, :], TOK_BANK[:, :]).then_inc(ytok_kept, 1)

            def gelu(e, q, k):
                act.wait_ge(hid_psum, q + k + 1)
                nc.scalar.activation(hid[k][:, :], H_BANK[k % (3 if e else 2)][:, :], ACT.Gelu_apprx_tanh,
                                     bias=b1c[e][:, k:k + 1]).then_inc(hid_ready, 1)

            def clean_body(t, first, last):
                gelu(0, FC * t, 0)
                gelu(0, FC * t, 1)
                act.wait_ge(logT_psum, t + 1)
                nc.scalar.copy(logT[:, :], L_BANK[:, 0:P]).then_inc(logT_ready, 1)
                if not last:
                    cnt_copy(2 * t + 1, 0)
                if not first:
                    ytok_keep(t - 1)
                gelu(0, FC * t, 2)
                act.wait_ge(z_psum, t + 1)
                raw = L_BANK[:, P:2 * P].rearrange("p (g w) -> p g w", g=SUB)[:, :, 0:E]
                nc.scalar.copy(z_all[:, bass.ds(t * SUB, SUB), :], raw).then_inc(z_raw_ready, 1)
                if not last:
                    cnt_copy(2 * t + 1, 1)
                gelu(0, FC * t, 3)
                if not last:
                    cnt_copy(2 * t + 2, 0)
                    act.wait_ge(xnT_kept, t + 1)
                    xnT_copy(t + 1)
                    nc.scalar.copy(xnTh[:, :], X_BANK[:, :]).then_inc(xnTh_step, 1)
                    cnt_copy(2 * t + 2, 1)
                act.wait_ge(hid_used, FC * (t + 1))
                nc.scalar.activation(yT[0][:, :], Y_BANK[0][:, :], ACT.Identity,
                                     bias=b2c[0][:, 0:1]).then_inc(y_ready, 1)

            def perturbed_body(t, last):
                for k in range(FC):
                    gelu(1, FC * (t + NT), k)
                if last:
                    act.wait_ge(xnT_kept, NT)
                    xnT_copy(NT)
                act.wait_ge(hid_used, FC * (t + NT + 1))
                nc.scalar.activation(yT[1][:, :], Y_BANK[1][:, :], ACT.Identity,
                                     bias=b2c[1][:, 0:1]).then_inc(y_ready, 1)

            def features(i, p):
                for a, (src, dst) in enumerate(((Q_BANK, qf), (KEY_BANK, kf))):
                    act.wait_ge(feat_psum, 2 * PAIRS * i + 2 * p + a + 1)
                    if p >= 2 and a == 0:
                        act.wait_ge(score_psum, COMBOS * i + 4 * (p - 1))
                    nc.scalar.activation(dst[p % 2][:, :], src[:, :], ACT.Relu).then_inc(feat_ready, 1)

            def qk_high(i, a, first):
                act.wait_ge(qk_psum, 2 * i + a + 1)
                if not first:
                    for g in range(GROUPS):
                        act.wait_ge(stacked[g], 16 * COPIES * i)
                nc.scalar.activation(qk_part[0][:, a, :], X_BANK[:, :], ACT.Identity,
                                     bias=bqk_sb[:, a:a + 1]).then_inc(qk_high_ready, 1)

            def ctx_copy(i, g):
                act.wait_ge(aw_used, BATCHES * i + NSEQ * (g + 1))
                nc.scalar.copy(ctxT[g % 2][:, :], C_BANK[:, :]).then_inc(ctxT_ready, 1)

            def ctxn_copy(i):
                act.wait_ge(ctxnT_psum, i + 1)
                nc.scalar.copy(ctxnT[:, :], T_BANK[:, :]).then_inc(ctxnT_ready, 1)

            def attn_body(i, n, first, last):
                for p in range(1, PAIRS):
                    features(i, p)
                    if p == 2 and not first:
                        ctxn_copy(i - 1)
                    if p >= 3 and p % 2 == 1:
                        ctx_copy(i, (p - 3) // 2)
                    if p == 4:
                        xnT_copy(n + 1)
                    if p in (5, 6) and not last:
                        qk_high(i + 1, p - 5, False)
                if not last:
                    features(i + 1, 0)
                ctx_copy(i, GROUPS - 1)

            act.wait_ge(b_loaded, 16 * N_B)
            nc.scalar.activation(gelu_warm[:, :], b2c[0][:, :], ACT.Gelu_apprx_tanh)
            xnT_copy(0)
            nc.scalar.copy(xnTh[:, :], X_BANK[:, :]).then_inc(xnTh_step, 1)
            act.wait_ge(setup_psum, 1)
            nc.scalar.copy(wv_t[:, :], bk[0][:, 0:P]).then_inc(setup_copied, 1)
            nc.scalar.copy(wout_t[:, :], bk[0][:, P:2 * P]).then_inc(setup_copied, 1)
            qk_cols = bk[0][:, 2 * P:4 * P].rearrange("p (a o) -> p a o", a=2)
            nc.scalar.copy(wqk_h[:, :, :], qk_cols).then_inc(setup_copied, 1)
            nc.scalar.copy(wqk_t[:, :, :], qk_cols).then_inc(setup_copied, 1)
            for g in range(2):
                cnt_copy(0, g)
            clean_body(0, True, False)
            with act.Fori(1, NT - 1) as i:
                clean_body(i, False, False)
            clean_body(NT - 1, False, True)
            ytok_keep(NT - 1)
            act.wait_ge(b_ready, 1)
            with act.Fori(0, NT - 1) as i:
                perturbed_body(i, False)
            perturbed_body(NT - 1, True)
            act.wait_ge(cols_loaded, 16 * N_COLS)
            qk_high(0, 0, True)
            qk_high(0, 1, True)
            features(0, 0)
            attn_body(0, NT, True, False)
            with act.Fori(1, NT - 1) as i:
                attn_body(i, i + NT, False, False)
            attn_body(NT - 1, 2 * NT - 1, False, True)
            ctxn_copy(NT - 1)
            with act.Fori(0, NT) as i:
                ffn_body(i + NT, i + 2 * NT)

        @block.gpsimd
        def _(pool):
            nc.gpsimd.memset(proj_copies[:, :], 0.0).then_inc(proj_zeroed, 1)
            nc.gpsimd.memset(ident[:, :], 0.0).then_inc(const_step, 1)
            nc.gpsimd.memset(causal[:, :], 1.0).then_inc(const_step, 1)
            nc.gpsimd.memset(v_aug[:, :, :, :], 0.0).then_inc(const_step, 1)
            nc.gpsimd.memset(wr_g[:, :], 0.0).then_inc(const_step, 1)
            nc.gpsimd.memset(minus_half[:, :], -0.5).then_inc(const_step, 1)
            nc.gpsimd.memset(eps_tile[:, :], EPS).then_inc(const_step, 1)
            nc.gpsimd.memset(two[:, :, :], 2.0).then_inc(const_step, 1)
            nc.gpsimd.memset(ones16[:, :], 1.0).then_inc(const_step, 1)
            for g in range(2):
                for col, most in enumerate(RANKS):
                    nc.gpsimd.memset(minus_most[:, g, col:col + 1], -float(most // P)).then_inc(const_step, 1)
            pool.wait_ge(const_step, 12)
            for g in range(2):
                for col, most in enumerate(RANKS):
                    nc.gpsimd.memset(minus_most[0:most % P, g, col:col + 1],
                                     -float(most // P + 1)).then_inc(const_step, 1)
            nc.gpsimd.affine_select(out=ident[:, :], in_=ident[:, :], compare_op=ALU.not_equal, fill=1.0,
                                    base=0, pattern=[[-1, P]], channel_multiplier=1).then_inc(const_step, 1)
            for lo in (0, S):
                nc.gpsimd.affine_select(out=causal[:, lo:lo + P], in_=causal[:, lo:lo + P], compare_op=ALU.is_ge,
                                        fill=0.0, base=0, pattern=[[1, P]],
                                        channel_multiplier=-1).then_inc(const_step, 1)
            nc.gpsimd.memset(v_aug[:, :, :, D:D + 1], 1.0).then_inc(const_step, 1)
            pool.wait_ge(const_step, 20)
            nc.gpsimd.memset(etot[:, :], 0.0).then_inc(const_ready, 1)
            nc.gpsimd.memset(erec[:, :], 0.0).then_inc(y_added, 1)

            for b in range(BITS):
                nc.gpsimd.memset(bits[:, b:b + 1], 1 << (BITS - 1 - b))
                last = nc.gpsimd.memset(bits_f[:, b:b + 1], float(1 << (BITS - 1 - b)))
            last.then_inc(bits_ready, 1)

            def rstd_pow(n):
                pool.wait_ge(stats_ready, n + 1)
                step = Steps(pool, norm_step, 1 * n)
                step(nc.gpsimd.tensor_tensor(var_eps[:, :], mv[:, :, 1], eps_tile[:, :], ALU.add))
                nc.gpsimd.tensor_tensor(rstd[:, :], var_eps[:, :], minus_half[:, :], ALU.pow).then_inc(rstd_ready, 1)

            def second_norm(t, n, dst):
                pool.wait_ge(rstd_ready, n + 1)
                step = Steps(pool, ratio_step, 3 * t)
                step(nc.gpsimd.tensor_tensor(ratio[:, :], mv[:, :, 1], rstd[:, :], ALU.mult))
                step(nc.gpsimd.tensor_tensor(ratio[:, :], ratio[:, :], rstd[:, :], ALU.mult))
                step(nc.gpsimd.tensor_tensor(ratio[:, :], ratio[:, :], eps_tile[:, :], ALU.add))
                nc.gpsimd.tensor_tensor(dst, ratio[:, :], minus_half[:, :], ALU.pow).then_inc(rstd2_ready, 1)

            def ffn_body(t, n):
                second_norm(t, n, rstd2[:, :])
                rstd_pow(n + 1)
                pool.wait_ge(z_ready, t - NT + 1)
                nc.gpsimd.tensor_tensor(ez[:, :, :], two[:, :, :], z[:, :, :], ALU.pow).then_inc(ez_ready, 1)

            def attn_body(i, n):
                pool.wait_ge(xn_ready, n + 1)
                xt = x[:, bass.ds(i * SUB, SUB), :]
                nc.gpsimd.tensor_tensor(xt, xt, bout_rows[:, :].unsqueeze(1).to_broadcast([P, SUB, C]),
                                        ALU.add).then_inc(bout_added, 1)
                rstd_pow(n + 1)

            pool.wait_ge(w1_loaded, 16)
            nc.gpsimd.tensor_copy(w1h[0][:, :, :], w1[0][:, :, :]).then_inc(w1h_ready, 1)
            pool.wait_ge(w1h_ready, 1)
            nc.gpsimd.tensor_tensor(w1l[0][:, :, :], w1[0][:, :, :], w1h[0][:, :, :].bitcast(F32),
                                    ALU.subtract).then_inc(clean_ready, 1)
            rstd_pow(0)
            pool.wait_ge(w2_loaded, 16)
            for g, w in enumerate((w1, w2)):
                nc.gpsimd.tensor_scalar(scaled[g][:, :], w[0][:, :, :].rearrange("p c f -> p (c f)"), SCALE, None,
                                        ALU.mult).then_inc(scaled_ready, 1)

            def keep_xnT(t):
                pool.wait_ge(xnT_ready, t + 1)
                nc.gpsimd.tensor_copy(xnT_all[:, bass.ds(t, 1), :], xnT[:, :]).then_inc(xnT_kept, 1)

            with pool.Fori(0, NT - 1) as i:
                second_norm(i, i, rstd2_all[:, bass.ds(i * SUB, SUB)])
                keep_xnT(i)
                rstd_pow(i + 1)
            second_norm(NT - 1, NT - 1, rstd2_all[:, (NT - 1) * SUB:NT * SUB])
            keep_xnT(NT - 1)
            pool.wait_ge(bias_step, 4 + 2 * (FC + 1))
            step = Steps(pool, b_perturb_step, 0)
            for cols, clean, pert, few in ((slice(0, FC), b1c[0], b1c[1], changed(FF) - 1),
                                           (slice(FC, FC + 1), b2c[0], b2c[1], changed(C) - 1)):
                t_, s_ = b_tier[:, 0:clean.shape[1]], b_scaled[:, 0:clean.shape[1]]
                step(nc.gpsimd.tensor_scalar(t_, n_more[:, cols], float(few), -2.0, ALU.is_le, ALU.mult))
                step(nc.gpsimd.tensor_scalar(s_, n_less[:, cols], float(few), None, ALU.is_le))
                step(nc.gpsimd.tensor_tensor(t_, t_, s_, ALU.add))
                step(nc.gpsimd.tensor_scalar(s_, clean[:, :], SCALE, None, ALU.mult))
                step(nc.gpsimd.tensor_scalar(t_, t_, -1.0, None, ALU.max))
                step(nc.gpsimd.tensor_tensor(t_, t_, s_, ALU.mult))
                step(nc.gpsimd.tensor_tensor(pert[:, :], clean[:, :], t_, ALU.add))
            nc.gpsimd.memset(b_scaled[:, :], 0.0).then_inc(b_ready, 1)
            pool.wait_ge(z_all_ready, 1)
            with pool.Fori(0, NT) as i:
                nc.gpsimd.tensor_tensor(ez_all[:, bass.ds(i * SUB, SUB), :], two[:, :, :],
                                        z_all[:, bass.ds(i * SUB, SUB), :], ALU.pow).then_inc(ez_ready, 1)
            pool.wait_ge(cols_loaded, 16 * N_COLS)
            pool.wait_ge(proj_loaded, 16 * N_PROJ)
            nc.gpsimd.tensor_copy(proj_parts[:, :], proj_copies[:, :]).then_inc(proj_rounded, 1)
            pool.wait_ge(proj_rounded, 1)
            low = slice(P // 2, P)
            nc.gpsimd.tensor_tensor(proj_parts[low, :], proj_copies[low, :], proj_parts[low, :].bitcast(F32),
                                    ALU.subtract).then_inc(feat_w_ready, 1)
            pool.wait_ge(feat_w_ready, 1)
            pool.wait_ge(setup_copied, 4)
            nc.gpsimd.tensor_tensor(wqk_l[:, :, :], wqk_t[:, :, :], wqk_h[:, :, :].bitcast(F32),
                                    ALU.subtract).then_inc(feat_w_ready, 1)
            rstd_pow(NT)
            with pool.Fori(0, NT) as i:
                attn_body(i, i + NT)
            with pool.Fori(0, NT) as i:
                ffn_body(i + NT, i + 2 * NT)

        @block.vector
        def _(dve):
            V = nc.vector
            setup = Steps(dve, setup_step, 0)
            flat = "p c f -> p (c f)"

            def magnitude(dst, src):
                return V.tensor_scalar(dst.bitcast(I32), src.bitcast(I32), 0x7FFFFFFF, None, ALU.bitwise_and)

            for g in range(2):
                setup(V.memset(found[g][:, :], 0))
            for g, loaded in enumerate((w1_loaded, w2_loaded)):
                dve.wait_ge(loaded, 16)
                setup(magnitude(mag[g][:, :], (w1, w2)[g][0][:, :, :].rearrange(flat)))

            def compare(g):
                for col in range(2):
                    last = V.tensor_scalar(below[g][:, col, :], mag[g][:, :], trial[g][:, col:col + 1].bitcast(F32),
                                           None, ALU.is_lt)
                last.then_inc(mask_ready, 1)

            def accept(g, b, before):
                dve.wait_ge(tot_ready, before + 1)
                return V.tensor_scalar(keep[g][:, :], CNT_BANK[g][:, TOT:TOT + 2], 0.0, bits_f[:, bass.ds(b, 1)],
                                       ALU.is_le, ALU.mult)

            def stats_part(g, tile):
                V.bn_stats(bn6[:, g, :], x[:, bass.ds(tile * SUB + g, 1), :]).then_inc(stats_step, 1)

            def stats_end(n):
                dve.wait_ge(stats_step, SUB * (n + 1))
                V.memset(spare[:, :], 0.0)
                for g in range(SUB):
                    last = V.bn_aggr(mv[:, g, :], bn6[:, g, :])
                last.then_inc(stats_ready, 1)

            def stats(n, tile):
                for g in range(SUB):
                    stats_part(g, tile)
                stats_end(n)

            def rank_biases(chunks):
                for c in chunks:
                    one, every = (ab1[:, c:c + 1], ab1_row) if c < FC else (ab2[:, 0:1], ab2_row)
                    for way, (n_, op) in enumerate(((n_less, ALU.is_lt), (n_more, ALU.is_gt))):
                        V.tensor_scalar(compared[:, way, c, 0:every.shape[1]], every[:, :], one, None, op, ALU.add,
                                        accum_out=n_[:, c:c + 1]).then_inc(bias_step, 1)

            dve.wait_ge(x0_loaded, 16)
            stats(0, 0)
            dve.wait_ge(bits_ready, 1)
            step = Steps(dve, search_step, 0)
            for g in range(2):
                step(V.tensor_tensor(trial[g][:, :], found[g][:, :], bits[:, 0:1].to_broadcast([P, 2]), ALU.bitwise_or))
                compare(g)

            def decide(b, g):
                accept(g, b - 1, 2 * (b - 1) + g).then_inc(search_step, 1)

            def propose(b, g):
                dve.wait_ge(search_step, 6 * (b - 1) + 3 * g + 3)
                V.scalar_tensor_tensor(out=trial[g][:, :], in0=keep[g][:, :], scalar=bits[:, bass.ds(b, 1)],
                                       in1=found[g][:, :], op0=ALU.bitwise_or,
                                       op1=ALU.bitwise_or).then_inc(search_step, 1)

            def test(b, g):
                dve.wait_ge(search_step, 6 * (b - 1) + 3 * g + 4)
                compare(g)
                V.tensor_tensor(found[g][:, :], found[g][:, :], keep[g][:, :], ALU.bitwise_or).then_inc(search_step, 1)

            def search_end():
                step = Steps(dve, search_step, 6 * (BITS - 1) + 2)
                for g in range(2):
                    step(accept(g, BITS - 1, 2 * (BITS - 1) + g))
                    step(V.tensor_tensor(found[g][:, :], found[g][:, :], keep[g][:, :], ALU.bitwise_or))

            def normalise_part(g, tile):
                return V.tensor_scalar(xn[:, g, :], x[:, bass.ds(tile * SUB + g, 1), :], mv[:, g, 0:1],
                                       rstd[:, g:g + 1], ALU.subtract, ALU.mult)

            def normalise(n, tile):
                dve.wait_ge(rstd_ready, n + 1)
                for g in range(SUB):
                    last = normalise_part(g, tile)
                last.then_inc(xn_ready, 1)

            def split(src, step, count, split_ready):
                V.tensor_copy(xnTh[:, :], src).then_inc(step, 1)
                dve.wait_ge(step, count)
                V.tensor_tensor(xnTl[:, :], src, xnTh[:, :].bitcast(F32), ALU.subtract).then_inc(split_ready, 1)

            def split_xnT(n):
                dve.wait_ge(xnT_ready, n + 1)
                split(xnT[:, :], xnTh_step, n + 1, xnT_split)

            def add_expert(t, e, tile):
                dve.wait_ge(ytok_psum, 2 * t + e + 1)
                for g in range(SUB):
                    xt = x[:, bass.ds(tile * SUB + g, 1), :]
                    last = V.scalar_tensor_tensor(out=xt, in0=YTOK_BANK[:, g * P:(g + 1) * P],
                                                  scalar=prob[:, e, g:g + 1], in1=xt, op0=ALU.mult, op1=ALU.add)
                last.then_inc(y_added, 1)

            def probabilities(t, powers):
                dve.wait_ge(ez_ready, t + 1)
                step = Steps(dve, prob_step, 4 * t)
                step(V.tensor_reduce(esum[:, :], powers[:, :, 1:E], AX_X, ALU.add))
                step(V.tensor_tensor(etot[:, :], esum[:, :], powers[:, :, 0], ALU.add))
                step(V.reciprocal(erec[:, :], etot[:, :]))
                V.scalar_tensor_tensor(out=prob[:, 0, :], in0=powers[:, :, 0], scalar=0.5, in1=erec[:, :],
                                       op0=ALU.mult, op1=ALU.mult)
                step(V.scalar_tensor_tensor(out=prob[:, 1, :], in0=esum[:, :], scalar=0.5, in1=erec[:, :],
                                            op0=ALU.mult, op1=ALU.mult))

            def clean_body(t):
                decide(2 * t + 1, 0)
                dve.wait_ge(rstd2_ready, t + 1)
                stats_part(0, t + 1)
                propose(2 * t + 1, 0)
                stats_part(1, t + 1)
                test(2 * t + 1, 0)
                stats_part(2, t + 1)
                stats_part(3, t + 1)
                stats_end(t + 1)
                decide(2 * t + 1, 1)
                propose(2 * t + 1, 1)
                test(2 * t + 1, 1)
                dve.wait_ge(xnT_psum, t + 1)
                decide(2 * t + 2, 0)
                dve.wait_ge(rstd_ready, t + 2)
                normalise_part(0, t + 1)
                propose(2 * t + 2, 0)
                normalise_part(1, t + 1)
                test(2 * t + 2, 0)
                decide(2 * t + 2, 1)
                normalise_part(2, t + 1)
                propose(2 * t + 2, 1)
                normalise_part(3, t + 1).then_inc(xn_ready, 1)
                test(2 * t + 2, 1)
                low_part(t + 1)

            def low_part(n):
                dve.wait_ge(xnTh_step, n + 1)
                V.tensor_tensor(xnTl[:, :], xnT[:, :], xnTh[:, :].bitcast(F32), ALU.subtract).then_inc(xnT_split, 1)

            def logits_shifted():
                dve.wait_ge(z_raw_ready, NT)
                dve.wait_ge(rstd2_ready, NT)
                step = Steps(dve, z_all_step, 0)
                za = z_all[:, :, :]
                step(V.tensor_tensor(za, za, rstd2_all[:, :].unsqueeze(2).to_broadcast([P, G, E]), ALU.mult))
                step(V.tensor_tensor(za, za, logit_b[:, :].unsqueeze(1).to_broadcast([P, G, E]), ALU.add))
                step(V.tensor_reduce(zmax_all[:, :], za, AX_X, ALU.max))
                V.tensor_tensor(za, za, zmax_all[:, :].unsqueeze(2).to_broadcast([P, G, E]),
                                ALU.subtract).then_inc(z_all_ready, 1)

            def split_again(t):
                split(xnT_all[:, bass.ds(t, 1), :].rearrange("p a t -> p (a t)"), again_step, t + 1, xnT_split_again)

            def add_perturbed(t):
                dve.wait_ge(ytok_psum, NT + t + 1)
                dve.wait_ge(y_added, 2 * t + 2)
                for g in range(SUB):
                    xt = x[:, bass.ds(t * SUB + g, 1), :]
                    last = V.scalar_tensor_tensor(out=xt, in0=YTOK_BANK[:, g * P:(g + 1) * P],
                                                  scalar=prob[:, 1, g:g + 1], in1=xt, op0=ALU.mult, op1=ALU.add)
                last.then_inc(y_added, 1)

            def perturbed_body(t, first, last):
                if last:
                    stats(NT, 0)
                if not first:
                    add_perturbed(t - 1)
                if last:
                    dve.wait_ge(xnT_psum, NT)
                    normalise(NT, 0)
                probabilities(t, ez_all[:, bass.ds(t * SUB, SUB), :])
                dve.wait_ge(hid_psum, FC * (t + NT + 1))
                if last:
                    split_xnT(NT)
                else:
                    split_again(t + 1)
                for g in range(SUB):
                    xt = x[:, bass.ds(t * SUB + g, 1), :]
                    done = V.scalar_tensor_tensor(out=xt, in0=ytok_all[:, bass.ds(t, 1), g, :],
                                                  scalar=prob[:, 0, g:g + 1], in1=xt, op0=ALU.mult, op1=ALU.add)
                done.then_inc(y_added, 1)

            def ffn_body(t, n, tile, following, before):
                if before is not None:
                    add_expert(t - 1, 1, before)
                dve.wait_ge(rstd2_ready, t + 1)
                stats(n + 1, following)
                dve.wait_ge(z_psum, t + 1)
                step = Steps(dve, z_step, 3 * (t - NT))
                raw = L_BANK[:, P:2 * P].rearrange("p (g w) -> p g w", g=SUB)[:, :, 0:E]
                step(V.tensor_tensor(z[:, :, :], raw, rstd2[:, :].unsqueeze(2).to_broadcast([P, SUB, E]), ALU.mult))
                step(V.tensor_tensor(z[:, :, :], z[:, :, :], logit_b[:, :].unsqueeze(1).to_broadcast([P, SUB, E]),
                                     ALU.add))
                step(V.tensor_reduce(zmax[:, :], z[:, :, :], AX_X, ALU.max))
                V.tensor_tensor(z[:, :, :], z[:, :, :], zmax[:, :].unsqueeze(2).to_broadcast([P, SUB, E]),
                                ALU.subtract).then_inc(z_ready, 1)
                dve.wait_ge(xnT_psum, n + 1)
                normalise(n + 1, following)
                probabilities(t, ez[:, :, :])
                dve.wait_ge(hid_psum, K2 * (t + 1))
                split_xnT(n + 1)
                add_expert(t, 0, tile)

            def scores_masked(i, m, first):
                dve.wait_ge(score_psum, COMBOS * i + m + 1)
                g, b = m // (2 * HG), m // 2 % 2
                if g >= 2 or not first:
                    dve.wait_ge(aw_used, BATCHES * i + NSEQ * (g - 2) + b + 1)
                V.tensor_tensor(aw[m % AW_BUFS][:, :], S_BANK[m % 3][:, 0:AW], causal[:, :],
                                ALU.mult).then_inc(aw_ready, 1)

            def ctx_normalised(i, g):
                dve.wait_ge(ctok_psum, GROUPS * i + g + 1)
                raw = T_BANK[:, :].rearrange("p (s j w) -> p s j w", s=SUB, j=HG)
                step = Steps(dve, norm_ctx_step, 2 * (GROUPS * i + g))
                step(V.tensor_scalar(den[:, :, :], raw[:, :, :, D], DELTA, None, ALU.add))
                step(V.reciprocal(rden[:, :, :], den[:, :, :]))
                part = ctxn[:, :, g * HG * D:(g + 1) * HG * D].rearrange("p s (j d) -> p s j d", j=HG)
                V.tensor_tensor(part, raw[:, :, :, 0:D], rden[:, :, :].unsqueeze(3).to_broadcast([P, SUB, HG, D]),
                                ALU.mult).then_inc(ctxn_ready, 1)

            def attn_finished(i, tile):
                dve.wait_ge(attn_psum, i + 1)
                dve.wait_ge(bout_added, i + 1)
                xt = x[:, bass.ds(tile * SUB, SUB), :]
                V.tensor_tensor(xt, X_BANK[:, :].rearrange("p (s c) -> p s c", s=SUB), xt,
                                ALU.add).then_inc(attn_added, 1)

            def qk_low(i, a):
                dve.wait_ge(qk_high_ready, 2 * i + a + 1)
                V.scalar_tensor_tensor(out=qk_part[1][:, a, :], in0=X_BANK[:, :], scalar=bqk_sb[:, a:a + 1],
                                       in1=qk_part[0][:, a, :].bitcast(F32), op0=ALU.add,
                                       op1=ALU.subtract).then_inc(qk_low_ready, 1)

            def values(i, first):
                dve.wait_ge(v_psum, i + 1)
                if not first:
                    dve.wait_ge(aw_used, BATCHES * i)
                bias = bv_rows[:, :].rearrange("p (h d) -> p h d", h=H).unsqueeze(1).to_broadcast([P, SUB, H, D])
                V.tensor_tensor(v_aug[:, :, :, 0:D], X_BANK[:, :].rearrange("p (s h d) -> p s h d", s=SUB, h=H), bias,
                                ALU.add).then_inc(v_ready, 1)

            def attn_body(i, n, following, before, last):
                first = before is None
                for s in range(STEPS):
                    scores_masked(i, 2 * s, first)
                    scores_masked(i, 2 * s + 1, first)
                    if s == 0:
                        values(i, first)
                    if s == 1 and not first:
                        ctx_normalised(i - 1, GROUPS - 1)
                    if s == 2:
                        stats(n + 1, following)
                    if s == 4 and not first:
                        attn_finished(i - 1, before)
                    if s == 5:
                        dve.wait_ge(xnT_psum, n + 1)
                        normalise(n + 1, following)
                    if s >= 6 and s % 4 == 2:
                        ctx_normalised(i, (s - 6) // 4)
                    if s == 8:
                        split_xnT(n + 1)
                    if s in (10, 12) and not last:
                        qk_low(i + 1, s // 2 - 5)

            normalise(0, 0)
            dve.wait_ge(const_ready, 1)
            dve.wait_ge(w_loaded, 16 * N_W)
            dve.wait_ge(cols_loaded, 16 * N_COLS)
            setup(V.tensor_scalar(wr_g[:, 0:E], wr_sb[:, :], gamma_sb[:, 0:1], LOG2E, ALU.mult, ALU.mult))
            setup(V.tensor_scalar(wr_l[:, :], wr_sb[:, :], LOG2E, None, ALU.mult))
            setup(V.tensor_copy(beta_wide[:, :], beta_sb[:, 0:1].to_broadcast([P, P])))
            dve.wait_ge(b_loaded, 16 * N_B)
            for dst, src in ((ab1, b1c[0]), (ab2, b2c[0]), (ab1_row, ab1_row), (ab2_row, ab2_row)):
                magnitude(dst[:, :], src[:, :]).then_inc(bias_step, 1)
            dve.wait_ge(bias_step, 4)
            rank_biases(range(1))
            low_part(0)
            dve.wait_ge(logit_b_psum, 1)
            V.scalar_tensor_tensor(out=logit_b[:, :], in0=br_rows[:, :], scalar=LOG2E, in1=bk[1][:, 64:64 + E],
                                   op0=ALU.mult, op1=ALU.add).then_inc(logit_b_copied, 1)

            rank_biases(range(1, FC + 1))
            dve.wait_ge(x1_loaded, 16)
            clean_body(0)
            dve.wait_ge(x_loaded, 16 * N_X)
            with dve.Fori(1, NT - 1) as i:
                clean_body(i)
            search_end()

            step = Steps(dve, perturb_step, 0)
            def perturb_matrix(g, w):
                step(V.tensor_scalar(tier[:, :], mag[g][:, :], found[g][:, 1:2].bitcast(F32), -2.0, ALU.is_ge,
                                     ALU.mult))
                step(V.scalar_tensor_tensor(out=tier[:, :], in0=mag[g][:, :], scalar=found[g][:, 0:1].bitcast(F32),
                                            in1=tier[:, :], op0=ALU.is_le, op1=ALU.add))
                step(V.scalar_tensor_tensor(out=tier[:, :], in0=tier[:, :], scalar=-1.0, in1=scaled[g][:, :],
                                            op0=ALU.max, op1=ALU.mult))
                step(V.tensor_tensor(w[1][:, :, :].rearrange(flat), w[0][:, :, :].rearrange(flat), tier[:, :], ALU.add))

            dve.wait_ge(scaled_ready, 2)
            perturb_matrix(0, w1)
            V.tensor_copy(w1h[1][:, :, :], w1[1][:, :, :]).then_inc(w1h_p_ready, 1)
            dve.wait_ge(w1h_p_ready, 1)
            V.tensor_tensor(w1l[1][:, :, :], w1[1][:, :, :], w1h[1][:, :, :].bitcast(F32),
                            ALU.subtract).then_inc(weights_ready, 1)
            logits_shifted()
            dve.wait_ge(hid_psum, FC * NT)
            split_again(0)
            perturb_matrix(1, w2)
            V.memset(spare[:, :], 0.0).then_inc(weights_ready, 1)
            perturbed_body(0, True, False)
            with dve.Fori(1, NT - 1) as i:
                perturbed_body(i, False, False)
            perturbed_body(NT - 1, False, True)
            qk_low(0, 0)
            add_perturbed(NT - 1)
            qk_low(0, 1)
            attn_body(0, NT, 1, None, False)
            with dve.Fori(1, NT - 1) as i:
                attn_body(i, i + NT, i + 1, i - 1, False)
            attn_body(NT - 1, 2 * NT - 1, 0, NT - 2, True)
            ctx_normalised(NT - 1, GROUPS - 1)
            attn_finished(NT - 1, NT - 1)
            ffn_body(NT, 2 * NT, 0, 1, None)
            with dve.Fori(1, NT) as i:
                ffn_body(i + NT, i + 2 * NT, i, (i + 1) % NT, i - 1)
            add_expert(2 * NT - 1, 1, NT - 1)

        @block.tensor
        def _(pe):
            mm = nc.tensor.matmul
            pe.wait_ge(const_ready, 1)

            def count(b, g):
                pe.wait_ge(mask_ready, 2 * b + g + 1)
                for col in range(2):
                    for c in range(FC):
                        last = mm(CNT_BANK[g][:, col:col + 1], below[g][:, col, c * P:(c + 1) * P],
                                  ones16[:, 0:1], start=(c == 0), stop=(c == FC - 1))
                last.then_inc(cnt_psum, 1)

            def total(b, g):
                pe.wait_ge(cnt_ready, 2 * b + g + 1)
                totals = CNT_BANK[g][:, TOT:TOT + 2]
                mm(totals, ones16[:, :], minus_most[:, g, :], start=True, stop=False)
                mm(totals, ones16[:, :], cnt[g][:, :], start=False, stop=True).then_inc(tot_ready, 1)

            def xn_transposed(n):
                pe.wait_ge(xn_ready, n + 1)
                for g in range(SUB):
                    last = nc.tensor.transpose(X_BANK[:, g * P:(g + 1) * P], xn[:, g, :], ident[:, :])
                last.then_inc(xnT_psum, 1)

            def mm3(dst, wh, wl):
                mm(dst, wh, xnTh[:, :], start=True, stop=False)
                mm(dst, wh, xnTl[:, :], start=False, stop=False)
                return mm(dst, wl, xnTh[:, :], start=False, stop=True)

            def y_transposed(t, e):
                pe.wait_ge(y_ready, 2 * t + e + 1)
                pe.wait_ge(y_added, 2 * t + e + 1)
                for g in range(SUB):
                    last = nc.tensor.transpose(YTOK_BANK[:, g * P:(g + 1) * P], yT[e][:, g * P:(g + 1) * P],
                                               ident[:, :])
                last.then_inc(ytok_psum, 1)

            def logits():
                for g in range(SUB):
                    last = mm(L_BANK[g * VW:(g + 1) * VW, 0:P], wr_g[:, :], xnT[:, g * P:(g + 1) * P], start=True,
                              stop=True, tile_position=(0, g * VW))
                last.then_inc(logT_psum, 1)

            def clean_transposed(t):
                pe.wait_ge(y_ready, t + 1)
                for g in range(SUB):
                    last = nc.tensor.transpose(TOK_BANK[:, g * P:(g + 1) * P], yT[0][:, g * P:(g + 1) * P], ident[:, :])
                last.then_inc(ytok_psum, 1)

            def clean_body(t, first, last):
                def hidden(k):
                    if k >= 2:
                        pe.wait_ge(hid_ready, FC * t + k - 1)
                    mm3(H_BANK[k % 2][:, :], w1h[0][:, k, :], w1l[0][:, k, :]).then_inc(hid_psum, 1)

                def output(k):
                    pe.wait_ge(hid_ready, FC * t + k + 1)
                    mm(Y_BANK[0][:, :], w2[0][:, k, :], hid[k][:, :], start=(k == 0),
                       stop=(k == FC - 1)).then_inc(hid_used, 1)

                pe.wait_ge(xnT_split, t + 1)
                hidden(0)
                hidden(1)
                logits()
                if not last:
                    count(2 * t + 1, 0)
                if not first:
                    clean_transposed(t - 1)
                hidden(2)
                if not last:
                    total(2 * t + 1, 0)
                pe.wait_ge(logT_ready, t + 1)
                nc.tensor.transpose(L_BANK[:, P:2 * P], logT[:, :], ident[:, :]).then_inc(z_psum, 1)
                output(0)
                if not last:
                    count(2 * t + 1, 1)
                hidden(3)
                if not last:
                    total(2 * t + 1, 1)
                output(1)
                if not last:
                    count(2 * t + 2, 0)
                    xn_transposed(t + 1)
                    total(2 * t + 2, 0)
                output(2)
                if not last:
                    count(2 * t + 2, 1)
                output(3)
                if not last:
                    total(2 * t + 2, 1)

            def perturbed_body(t, first, last):
                def hidden(k):
                    if k == 3:
                        pe.wait_ge(hid_ready, FC * (t + NT) + 1)
                    mm3(H_BANK[k % 3][:, :], w1h[1][:, k, :], w1l[1][:, k, :]).then_inc(hid_psum, 1)

                def output(k):
                    pe.wait_ge(hid_ready, FC * (t + NT) + k + 1)
                    mm(Y_BANK[1][:, :], w2[1][:, k, :], hid[k][:, :], start=(k == 0),
                       stop=(k == FC - 1)).then_inc(hid_used, 1)

                pe.wait_ge(xnT_split_again, t + 1)
                hidden(0)
                hidden(1)
                if not first:
                    perturbed_transposed(t - 1)
                hidden(2)
                if first:
                    hidden(3)
                    pe.wait_ge(weights_ready, 2)
                    output(0)
                else:
                    output(0)
                    hidden(3)
                output(1)
                if last:
                    xn_transposed(NT)
                output(2)
                output(3)

            def perturbed_transposed(t):
                pe.wait_ge(y_ready, NT + t + 1)
                pe.wait_ge(y_added, 2 * t + 1)
                for g in range(SUB):
                    cols = slice(g * P, (g + 1) * P)
                    last = nc.tensor.transpose(YTOK_BANK[:, cols], yT[1][:, cols], ident[:, :])
                last.then_inc(ytok_psum, 1)

            def ffn_body(t, n, first):
                def hidden(k):
                    e, c = divmod(k, FC)
                    if k >= 3:
                        pe.wait_ge(hid_ready, K2 * t + k - 2)
                    mm3(H_BANK[k % 3][:, :], w1h[e][:, c, :], w1l[e][:, c, :]).then_inc(hid_psum, 1)

                def output(k):
                    e, c = divmod(k, FC)
                    pe.wait_ge(hid_ready, K2 * t + k + 1)
                    last = mm(Y_BANK[e][:, :], w2[e][:, c, :], hid[k % 4][:, :], start=(c == 0), stop=(c == FC - 1))
                    last.then_inc(hid_used, 1)

                pe.wait_ge(xnT_split, n + 1)
                hidden(0)
                hidden(1)
                logits()
                if not first:
                    y_transposed(t - 1, 1)
                hidden(2)
                output(0)
                pe.wait_ge(logT_ready, t + 1)
                nc.tensor.transpose(L_BANK[:, P:2 * P], logT[:, :], ident[:, :]).then_inc(z_psum, 1)
                for k in range(3, K2):
                    hidden(k)
                    if k == 5:
                        xn_transposed(n + 1)
                    output(k - 2)
                    if k == 6:
                        y_transposed(t, 0)
                output(6)
                output(7)

            def ctx_transposed(i, g):
                pe.wait_ge(ctxT_ready, GROUPS * i + g + 1)
                if g >= 1:
                    pe.wait_ge(ctxn_ready, GROUPS * i + g)
                for s in range(SUB):
                    last = nc.tensor.transpose(T_BANK[:, s * P:(s + 1) * P], ctxT[g % 2][:, s * P:(s + 1) * P],
                                               ident[:, :])
                last.then_inc(ctok_psum, 1)

            def ctxn_transposed(i):
                pe.wait_ge(ctxn_ready, GROUPS * (i + 1))
                for s in range(SUB):
                    last = nc.tensor.transpose(T_BANK[:, s * P:(s + 1) * P], ctxn[:, s, :], ident[:, :])
                last.then_inc(ctxnT_psum, 1)

            def projected(i):
                pe.wait_ge(ctxnT_ready, i + 1)
                for s in range(SUB):
                    last = mm(X_BANK[:, s * P:(s + 1) * P], ctxnT[:, s * P:(s + 1) * P], wout_t[:, :],
                              start=True, stop=True)
                last.then_inc(attn_psum, 1)

            def qk_projected(i, a):
                if a == 1:
                    pe.wait_ge(qk_low_ready, 2 * i + 1)
                mm3(X_BANK[:, :], wqk_h[:, a, :], wqk_l[:, a, :]).then_inc(qk_psum, 1)

            def features(i, p, first):
                if p % 2 == 0:
                    pe.wait_ge(stacked[p // 2], 16 * COPIES * (i + 1))
                if p >= 1 or not first:
                    pe.wait_ge(feat_ready, 2 * (PAIRS * i + p))
                for a, dst in enumerate((Q_BANK, KEY_BANK)):
                    mm(dst[:, :], proj_parts[:, p * P:(p + 1) * P], qk_stack[:, a, p // 2, :], start=True,
                       stop=True).then_inc(feat_psum, 1)

            def v_projected(i):
                pe.wait_ge(qk_low_ready, 2 * (i + 1))
                for s in range(SUB):
                    cols = slice(s * P, (s + 1) * P)
                    last = mm(X_BANK[:, cols], xnT[:, cols], wv_t[:, :], start=True, stop=True)
                last.then_inc(v_psum, 1)

            def scores(i, s):
                p, b = divmod(s, NSEQ)
                if b == 0:
                    pe.wait_ge(feat_ready, 2 * (PAIRS * i + p + 1))
                q, k = qf[p % 2], kf[p % 2]
                t0, t1, t2 = b * S, b * S + P, (b + 1) * S
                for half in range(2):
                    for e in range(2):
                        m = 2 * s + e
                        if half == 0 and m >= 3:
                            pe.wait_ge(aw_ready, COMBOS * i + m - 2)
                        rows = slice(e * M, (e + 1) * M)
                        if half == 0:
                            mm(S_BANK[m % 3][:, 0:S], k[rows, t0:t1], q[rows, t0:t2], start=True, stop=True)
                        else:
                            mm(S_BANK[m % 3][:, S:AW], k[rows, t1:t2], q[rows, t1:t2], start=True,
                               stop=True).then_inc(score_psum, 1)

            def context(i, g, b):
                if g == 0 and b == 0:
                    pe.wait_ge(v_ready, i + 1)
                if g > 0 and b == 0:
                    pe.wait_ge(ctxT_ready, GROUPS * i + g)
                pe.wait_ge(aw_ready, COMBOS * i + 2 * HG * g + 2 * b + 6)
                for half in range(2):
                    for j in (1, 2, 3, 0):
                        scored = aw[(2 * HG * g + 4 * (j // 2) + 2 * b + j % 2) % AW_BUFS]
                        keys = v_aug[:, 2 * b + half, HG * g + j, :]
                        rows = slice(j * VW, (j + 1) * VW)
                        if half == 0:
                            mm(C_BANK[rows, b * S:(b + 1) * S], keys, scored[:, 0:S], start=True, stop=False,
                               tile_position=(0, j * VW))
                        else:
                            last = mm(C_BANK[rows, b * S + P:(b + 1) * S], keys, scored[:, S:AW], start=False,
                                      stop=True, tile_position=(0, j * VW))
                last.then_inc(aw_used, 1)

            def attn_body(i, n, first, last):
                for s in range(STEPS):
                    p, b = divmod(s, NSEQ)
                    if b == 0 and p + 1 < PAIRS:
                        features(i, p + 1, first)
                    scores(i, s)
                    if s % 4 == 3 and s < STEPS - 1:
                        context(i, s // 4, 0)
                    if s > 0 and s % 4 == 0:
                        context(i, s // 4 - 1, 1)
                    if not first:
                        if s == 1:
                            ctx_transposed(i - 1, GROUPS - 1)
                        if s == 2:
                            ctxn_transposed(i - 1)
                        if s == 3:
                            pe.wait_ge(v_ready, i + 1)
                            projected(i - 1)
                    if s >= 5 and s % 4 == 1:
                        ctx_transposed(i, (s - 5) // 4)
                    if s == 6:
                        if first:
                            pe.wait_ge(v_ready, 1)
                        else:
                            pe.wait_ge(attn_added, i)
                        xn_transposed(n + 1)
                    if s == 9 and not last:
                        pe.wait_ge(xnT_split, n + 2)
                        qk_projected(i + 1, 0)
                    if s == 11 and not last:
                        qk_projected(i + 1, 1)
                context(i, GROUPS - 1, 0)
                if not last:
                    features(i + 1, 0, False)
                    v_projected(i + 1)
                context(i, GROUPS - 1, 1)

            xn_transposed(0)
            pe.wait_ge(w_loaded, 16 * N_W)
            nc.tensor.transpose(bk[0][:, 0:P], wqkv_sb[:, 2, :], ident[:, :])
            nc.tensor.transpose(bk[0][:, P:2 * P], wout_sb[:, :], ident[:, :])
            for a in range(2):
                last = nc.tensor.transpose(bk[0][:, (2 + a) * P:(3 + a) * P], wqkv_sb[:, a, :], ident[:, :])
            last.then_inc(setup_psum, 1)
            pe.wait_ge(setup_step, 7)
            mm(bk[1][:, 64:64 + E], beta_wide[:, :], wr_l[:, :], start=True, stop=True).then_inc(logit_b_psum, 1)
            pe.wait_ge(clean_ready, 1)
            pe.wait_ge(setup_copied, 4)
            pe.wait_ge(logit_b_copied, 1)
            for g in range(2):
                count(0, g)
                total(0, g)
            clean_body(0, True, False)
            with pe.Fori(1, NT - 1) as i:
                clean_body(i, False, False)
            clean_body(NT - 1, False, True)
            clean_transposed(NT - 1)
            pe.wait_ge(weights_ready, 1)
            pe.wait_ge(ytok_kept, NT)
            perturbed_body(0, True, False)
            with pe.Fori(1, NT - 1) as i:
                perturbed_body(i, False, False)
            perturbed_body(NT - 1, False, True)
            pe.wait_ge(feat_w_ready, 2)
            pe.wait_ge(xnT_split, NT + 1)
            qk_projected(0, 0)
            perturbed_transposed(NT - 1)
            qk_projected(0, 1)
            pe.wait_ge(y_added, 2 * NT + 1)
            features(0, 0, True)
            v_projected(0)
            attn_body(0, NT, True, False)
            with pe.Fori(1, NT - 1) as i:
                attn_body(i, i + NT, False, False)
            attn_body(NT - 1, 2 * NT - 1, False, True)
            ctx_transposed(NT - 1, GROUPS - 1)
            ctxn_transposed(NT - 1)
            projected(NT - 1)
            pe.wait_ge(attn_added, NT)
            ffn_body(NT, 2 * NT, True)
            with pe.Fori(1, NT) as i:
                ffn_body(i + NT, i + 2 * NT, False)
            y_transposed(2 * NT - 1, 1)


_INS = ["L0_attn_x", "L0_attn_Wqkv", "L0_attn_bqkv", "L0_attn_Wout", "L0_attn_bout", "L0_attn_proj", "L0_ffn_W1",
        "L0_ffn_b1", "L0_ffn_W2", "L0_ffn_b2", "L0_ffn_ln_gamma", "L0_ffn_ln_beta", "L0_ffn_Wr", "L0_ffn_br"]


def kernel(**inputs):
    import numpy as np
    import concourse.bacc as bacc
    from concourse.bass_utils import run_bass_kernel_spmd

    nc = bacc.Bacc("TRN2", target_bir_lowering=False, num_devices=1)
    arrays, args = {}, []
    for name in _INS:
        a = np.ascontiguousarray(inputs[name])
        arrays["in_" + name] = a
        args.append(nc.dram_tensor("in_" + name, a.shape, mybir.dt.from_np(a.dtype), kind="ExternalInput").ap())
    shape = arrays["in_L0_attn_x"].shape
    out = nc.dram_tensor("out_x", shape, F32, kind="ExternalOutput").ap()
    macaron_kernel(nc, *args, out)
    r = run_bass_kernel_spmd(nc, [arrays], core_ids=[0])
    return r.results[0]["out_x"]
```
